# Optimizing a Trainium2 kernel written in Bass

```python
import numpy as np
import jax
import jax.numpy as jnp

def _softmax(x, axis=-1):
    return jax.nn.softmax(x, axis=axis)

def _gelu(x):
    return jax.nn.gelu(x, approximate=True)

def _silu(x):
    return jax.nn.silu(x)

def _sigmoid(x):
    return jax.nn.sigmoid(x)

def _layernorm(x, axis=-1, eps=1e-05):
    m = jnp.mean(x, axis=axis, keepdims=True)
    v = jnp.var(x, axis=axis, keepdims=True)
    return (x - m) / jnp.sqrt(v + eps)

def _scatter_add(tgt, idx, src, axis=0):
    return tgt.at[idx].add(src)

def _segment_sum(src, seg, n):
    return jax.ops.segment_sum(src, seg, n)
kernel_name = 'mk_perceiver_d1_seqx_r4_4dd049'

def setup_inputs(seed: int=0):
    np.random.seed(seed)
    _w = jnp.asarray

    def _rec_inputs():
        import jax
        import jax.numpy as jnp
        _rk = jax.random.key(seed)
        x = -0.0003929 + 0.9999 * jax.random.normal(jax.random.fold_in(_rk, 1), (1, 256, 512), jnp.float32)
        _lenS = 256 - jax.random.randint(jax.random.fold_in(_rk, 7), (1,), 0, max(1, 256 // 4) + 1, jnp.int32)
        _lenS2 = 4096 - jax.random.randint(jax.random.fold_in(_rk, 8), (1,), 0, max(1, 4096 // 4) + 1, jnp.int32)
        _ctx_2048P = jax.random.normal(jax.random.fold_in(_rk, 11), (1, 16, 512), jnp.float32)
        _ctx_2048c = jax.random.dirichlet(jax.random.fold_in(_rk, 511), 0.3 * jnp.ones((16,), jnp.float32), (1, 4096))
        _ctx_2048t = jnp.einsum('bsk,bkd->bsd', _ctx_2048c, _ctx_2048P)
        _ctx_2048t = _ctx_2048t * jax.lax.rsqrt(jnp.mean(jnp.square(_ctx_2048t)) + 1e-12) * 0.953939
        ctx_2048 = -0.000514642 + 1.00011 * (_ctx_2048t + 0.3 * jax.random.normal(jax.random.fold_in(_rk, 611), (1, 4096, 512), jnp.float32))
        _validS = jnp.arange(256)[None, :] < _lenS[:, None]
        _validS2 = jnp.arange(4096)[None, :] < _lenS2[:, None]
        _causal = jnp.tril(jnp.ones((256, 256), dtype=bool))
        mask_BxS2_ik0 = jnp.where(jnp.broadcast_to(_validS2[:, :], (1, 4096)), 0, 1).astype(jnp.int32)
        return (x, ctx_2048, mask_BxS2_ik0)
    x, ctx_2048, mask_BxS2_ik0 = _rec_inputs()

    def _L0_xattn_setup():
        import jax, jax.numpy as jnp
        import numpy as np
        import math
        H = 512
        NH = 16
        HD = H // NH
        EPS_LN = 1e-05
        RES_SCALE_MAX = 0.3

        def _nan_clean(x, lim=10000.0):
            return jnp.nan_to_num(x, nan=0.0, posinf=lim, neginf=-lim)
        key = jax.random.key(seed)
        ks = jax.random.split(key, 12)
        B, S, T = (4, 512, 64)
        std = 1.0 / math.sqrt(H)
        return {'hidden_states': jax.random.normal(ks[0], (B, S, H), jnp.float32), 'audio_tokens': jax.random.normal(ks[1], (B, T, H), jnp.float32), 'attention_mask': jax.random.randint(ks[2], (B, T), 0, 2, jnp.int32), 'Wq': jax.random.normal(ks[3], (H, H), jnp.float32) * std, 'bq': jnp.zeros((H,), jnp.float32), 'Wk': jax.random.normal(ks[4], (H, H), jnp.float32) * std, 'bk': jnp.zeros((H,), jnp.float32), 'Wv': jax.random.normal(ks[5], (H, H), jnp.float32) * std, 'bv': jnp.zeros((H,), jnp.float32), 'Wo': jax.random.normal(ks[6], (H, H), jnp.float32) * std, 'bo': jnp.zeros((H,), jnp.float32), 'ln_gamma': jnp.ones((H,), jnp.float32), 'ln_beta': jnp.zeros((H,), jnp.float32), 'residual_scale': jnp.float32(0.05)}
    _L0_xattn_all = _L0_xattn_setup()
    _L0_xattn_in = {k: v for k, v in _L0_xattn_all.items() if k in ('Wq', 'bq', 'Wk', 'bk', 'Wv', 'bv', 'Wo', 'bo', 'ln_gamma', 'ln_beta', 'residual_scale')}
    del _L0_xattn_all

    def _L0_attn_setup():
        import jax, jax.numpy as jnp
        import numpy as np
        HID = 512
        H = 16
        QLR = 384
        KVLR = 128
        DN = 128
        DR = 64
        DV = 128
        DQ = DN + DR
        B = 2
        S = 512
        THETA = 10000.0
        EPS = 1e-06

        def rms_norm(x, w, eps=EPS):
            x32 = x.astype(jnp.float32)
            var = jnp.mean(x32 * x32, axis=-1, keepdims=True)
            return (w * (x32 * jax.lax.rsqrt(var + eps))).astype(x.dtype)

        def rotate_half(x):
            x1, x2 = jnp.split(x, 2, axis=-1)
            return jnp.concatenate((-x2, x1), axis=-1)

        def rope_tables(seq_len, dim, base=THETA):
            inv_freq = 1.0 / base ** (jnp.arange(0, dim, 2, dtype=jnp.float32) / dim)
            t = jnp.arange(seq_len, dtype=jnp.float32)
            freqs = jnp.outer(t, inv_freq)
            emb = jnp.concatenate((freqs, freqs), -1)
            return (jnp.cos(emb), jnp.sin(emb))
        key = jax.random.key(seed)
        ks = jax.random.split(key, 8)
        sd = lambda fan_in: 1.0 / np.sqrt(fan_in)
        return {'hidden_states': jax.random.normal(ks[0], (B, S, HID), jnp.float32), 'w_qa': jax.random.normal(ks[1], (QLR, HID), jnp.float32) * sd(HID), 'q_a_ln_w': jnp.ones((QLR,), jnp.float32), 'w_qb': jax.random.normal(ks[2], (H * DQ, QLR), jnp.float32) * sd(QLR), 'w_kva': jax.random.normal(ks[3], (KVLR + DR, HID), jnp.float32) * sd(HID), 'kv_a_ln_w': jnp.ones((KVLR,), jnp.float32), 'w_kvb': jax.random.normal(ks[4], (H * (DN + DV), KVLR), jnp.float32) * sd(KVLR), 'w_o': jax.random.normal(ks[5], (HID, H * DV), jnp.float32) * sd(H * DV)}
    _L0_attn_all = _L0_attn_setup()
    _L0_attn_in = {k: v for k, v in _L0_attn_all.items() if k in ('w_qa', 'q_a_ln_w', 'w_qb', 'w_kva', 'kv_a_ln_w', 'w_kvb', 'w_o')}
    del _L0_attn_all

    def _L0_ffn_setup():
        import jax, jax.numpy as jnp
        import numpy as np
        NUM_EXPERTS = 128
        NUM_KEPT = 48
        TOP_K = 8
        HIDDEN = 512
        INTER = 192
        CAP = 192
        BATCH, SEQ = (2, 256)
        key = jax.random.key(seed)
        k1, k2, k3, k4 = jax.random.split(key, 4)
        hidden_states = jax.random.normal(k1, (BATCH, SEQ, HIDDEN), jnp.float32)
        gate_weight = jax.random.normal(k2, (NUM_EXPERTS, HIDDEN), jnp.float32) * 0.02
        gate_up_proj = jax.random.normal(k3, (NUM_KEPT, 2 * INTER, HIDDEN), jnp.float32) * 0.02
        down_proj = jax.random.normal(k4, (NUM_KEPT, HIDDEN, INTER), jnp.float32) * 0.02
        o2n = -np.ones(NUM_EXPERTS, np.int32)
        o2n[np.arange(NUM_KEPT) * 2] = np.arange(NUM_KEPT, dtype=np.int32)
        old_to_new = jnp.asarray(o2n)
        return {'hidden_states': hidden_states, 'gate_weight': gate_weight, 'gate_up_proj': gate_up_proj, 'down_proj': down_proj, 'old_to_new': old_to_new}
    _L0_ffn_all = _L0_ffn_setup()
    _L0_ffn_in = {k: v for k, v in _L0_ffn_all.items() if k in ('gate_weight', 'gate_up_proj', 'down_proj', 'old_to_new')}
    del _L0_ffn_all
    return {'x': x, 'ctx_2048': ctx_2048, 'mask_BxS2_ik0': mask_BxS2_ik0, 'L0_xattn_Wq': _L0_xattn_in['Wq'], 'L0_xattn_bq': _L0_xattn_in['bq'], 'L0_xattn_Wk': _L0_xattn_in['Wk'], 'L0_xattn_bk': _L0_xattn_in['bk'], 'L0_xattn_Wv': _L0_xattn_in['Wv'], 'L0_xattn_bv': _L0_xattn_in['bv'], 'L0_xattn_Wo': _L0_xattn_in['Wo'], 'L0_xattn_bo': _L0_xattn_in['bo'], 'L0_xattn_ln_gamma': _L0_xattn_in['ln_gamma'], 'L0_xattn_ln_beta': _L0_xattn_in['ln_beta'], 'L0_xattn_residual_scale': _L0_xattn_in['residual_scale'], 'L0_attn_w_qa': _L0_attn_in['w_qa'], 'L0_attn_q_a_ln_w': _L0_attn_in['q_a_ln_w'], 'L0_attn_w_qb': _L0_attn_in['w_qb'], 'L0_attn_w_kva': _L0_attn_in['w_kva'], 'L0_attn_kv_a_ln_w': _L0_attn_in['kv_a_ln_w'], 'L0_attn_w_kvb': _L0_attn_in['w_kvb'], 'L0_attn_w_o': _L0_attn_in['w_o'], 'L0_ffn_gate_weight': _L0_ffn_in['gate_weight'], 'L0_ffn_gate_up_proj': _L0_ffn_in['gate_up_proj'], 'L0_ffn_down_proj': _L0_ffn_in['down_proj'], 'L0_ffn_old_to_new': _L0_ffn_in['old_to_new']}

def reference(x, ctx_2048, mask_BxS2_ik0, L0_xattn_Wq, L0_xattn_bq, L0_xattn_Wk, L0_xattn_bk, L0_xattn_Wv, L0_xattn_bv, L0_xattn_Wo, L0_xattn_bo, L0_xattn_ln_gamma, L0_xattn_ln_beta, L0_xattn_residual_scale, L0_attn_w_qa, L0_attn_q_a_ln_w, L0_attn_w_qb, L0_attn_w_kva, L0_attn_kv_a_ln_w, L0_attn_w_kvb, L0_attn_w_o, L0_ffn_gate_weight, L0_ffn_gate_up_proj, L0_ffn_down_proj, L0_ffn_old_to_new):
    import jax
    import jax.numpy as jnp

    def _L0_xattn_ref(hidden_states, audio_tokens, attention_mask, Wq, bq, Wk, bk, Wv, bv, Wo, bo, ln_gamma, ln_beta, residual_scale):
        import jax, jax.numpy as jnp
        import numpy as np
        import math
        H = 512
        NH = 16
        HD = H // NH
        EPS_LN = 1e-05
        RES_SCALE_MAX = 0.3

        def _nan_clean(x, lim=10000.0):
            return jnp.nan_to_num(x, nan=0.0, posinf=lim, neginf=-lim)
        B, S, _ = hidden_states.shape
        T = audio_tokens.shape[1]
        hs = _nan_clean(hidden_states).astype(jnp.float32)
        at = _nan_clean(audio_tokens).astype(jnp.float32)

        def proj(x, W, b, L):
            y = x @ W.T + b
            return y.reshape(B, L, NH, HD).transpose(0, 2, 1, 3)
        q = _nan_clean(proj(hs, Wq, bq, S))
        k = _nan_clean(proj(at, Wk, bk, T))
        v = _nan_clean(proj(at, Wv, bv, T))
        scale = max(math.sqrt(HD), 1e-08)
        scores = jnp.einsum('bhsd,bhtd->bhst', q, k) / scale
        scores = jnp.clip(scores, -50.0, 50.0)
        scores = jnp.nan_to_num(scores, nan=0.0, posinf=50.0, neginf=-50.0)
        attend = (attention_mask.astype(jnp.float32) > 0.5)[:, None, None, :]
        scores = jnp.where(attend, scores, -10000.0)
        scores = jnp.clip(scores, -50.0, 50.0)
        probs = jax.nn.softmax(scores, axis=-1)
        probs = jnp.nan_to_num(probs, nan=0.0, posinf=1.0, neginf=0.0)
        probs = probs / (probs.sum(axis=-1, keepdims=True) + 1e-08)
        ctx = jnp.einsum('bhst,bhtd->bhsd', probs, v)
        ctx = ctx.transpose(0, 2, 1, 3).reshape(B, S, H)
        delta = _nan_clean(ctx @ Wo.T + bo)
        rs = jnp.clip(residual_scale, 0.0, RES_SCALE_MAX)
        delta = rs * delta
        mu = delta.mean(axis=-1, keepdims=True)
        var = jnp.mean((delta - mu) ** 2, axis=-1, keepdims=True)
        delta = (delta - mu) / jnp.sqrt(var + EPS_LN) * ln_gamma + ln_beta
        return delta

    def _L0_attn_ref(hidden_states, w_qa, q_a_ln_w, w_qb, w_kva, kv_a_ln_w, w_kvb, w_o):
        import jax, jax.numpy as jnp
        import numpy as np
        HID = 512
        H = 16
        QLR = 384
        KVLR = 128
        DN = 128
        DR = 64
        DV = 128
        DQ = DN + DR
        B = 2
        S = 512
        THETA = 10000.0
        EPS = 1e-06

        def rms_norm(x, w, eps=EPS):
            x32 = x.astype(jnp.float32)
            var = jnp.mean(x32 * x32, axis=-1, keepdims=True)
            return (w * (x32 * jax.lax.rsqrt(var + eps))).astype(x.dtype)

        def rotate_half(x):
            x1, x2 = jnp.split(x, 2, axis=-1)
            return jnp.concatenate((-x2, x1), axis=-1)

        def rope_tables(seq_len, dim, base=THETA):
            inv_freq = 1.0 / base ** (jnp.arange(0, dim, 2, dtype=jnp.float32) / dim)
            t = jnp.arange(seq_len, dtype=jnp.float32)
            freqs = jnp.outer(t, inv_freq)
            emb = jnp.concatenate((freqs, freqs), -1)
            return (jnp.cos(emb), jnp.sin(emb))
        b, s, _ = hidden_states.shape
        scale = DQ ** (-0.5)
        cos, sin = rope_tables(s, DR)
        cq = rms_norm(hidden_states @ w_qa.T, q_a_ln_w)
        q = (cq @ w_qb.T).reshape(b, s, H, DQ).transpose(0, 2, 1, 3)
        q_nope, q_pe = (q[..., :DN], q[..., DN:])
        q_pe = q_pe * cos + rotate_half(q_pe) * sin
        ckv = hidden_states @ w_kva.T
        k_pe = ckv[..., KVLR:].reshape(b, s, 1, DR).transpose(0, 2, 1, 3)
        k_pe = k_pe * cos + rotate_half(k_pe) * sin
        ckv_l = rms_norm(ckv[..., :KVLR], kv_a_ln_w)
        kv = (ckv_l @ w_kvb.T).reshape(b, s, H, DN + DV).transpose(0, 2, 1, 3)
        k_nope, v = (kv[..., :DN], kv[..., DN:])
        q_full = jnp.concatenate([q_nope, q_pe], axis=-1)
        k_full = jnp.concatenate([k_nope, jnp.broadcast_to(k_pe, (b, H, s, DR))], axis=-1)
        scores = jnp.einsum('bhqd,bhkd->bhqk', q_full, k_full) * scale
        causal = jnp.triu(jnp.ones((s, s), dtype=bool), k=1)
        scores = jnp.where(causal, -jnp.inf, scores)
        attn = jax.nn.softmax(scores.astype(jnp.float32), axis=-1).astype(q_full.dtype)
        out = jnp.einsum('bhqk,bhkd->bhqd', attn, v)
        out = out.transpose(0, 2, 1, 3).reshape(b, s, H * DV)
        return out @ w_o.T

    def _L0_ffn_ref(hidden_states, gate_weight, gate_up_proj, down_proj, old_to_new):
        import jax, jax.numpy as jnp
        import numpy as np
        NUM_EXPERTS = 128
        NUM_KEPT = 48
        TOP_K = 8
        HIDDEN = 512
        INTER = 192
        CAP = 192
        BATCH, SEQ = (2, 256)
        B, S, H = hidden_states.shape
        x = hidden_states.reshape(-1, H)
        T = x.shape[0]
        logits = x @ gate_weight.T
        logits = jnp.where(old_to_new[None, :] == -1, -jnp.inf, logits)
        probs = jax.nn.softmax(logits.astype(jnp.float32), axis=-1).astype(logits.dtype)
        top_v, top_i = jax.lax.top_k(probs, TOP_K)
        top_v = top_v / jnp.sum(top_v, axis=-1, keepdims=True)
        sel_new = old_to_new[top_i]
        E = gate_up_proj.shape[0]
        flat_e = sel_new.reshape(-1)
        flat_w = top_v.reshape(-1)
        tok = jnp.repeat(jnp.arange(T), TOP_K)
        oh = (flat_e[:, None] == jnp.arange(E)[None, :]).astype(jnp.int32)
        pos = jnp.sum(jnp.cumsum(oh, axis=0) * oh, axis=-1) - 1
        valid = pos < CAP
        pos_c = jnp.where(valid, pos, CAP)
        xb = jnp.zeros((E, CAP + 1, H), x.dtype).at[flat_e, pos_c].set(x[tok])
        xb = xb[:, :CAP]
        gu = jnp.einsum('ech,eoh->eco', xb, gate_up_proj)
        g, u = jnp.split(gu, 2, axis=-1)
        h = jax.nn.silu(g) * u
        out = jnp.einsum('eci,ehi->ech', h, down_proj)
        y = out[flat_e, jnp.minimum(pos_c, CAP - 1)]
        w = flat_w * valid.astype(flat_w.dtype)
        final = jnp.zeros_like(x).at[tok].add(y * w[:, None])
        return final.reshape(B, S, H)
    x = x + _L0_xattn_ref(_layernorm(x, axis=-1), ctx_2048, mask_BxS2_ik0, L0_xattn_Wq, L0_xattn_bq, L0_xattn_Wk, L0_xattn_bk, L0_xattn_Wv, L0_xattn_bv, L0_xattn_Wo, L0_xattn_bo, L0_xattn_ln_gamma, L0_xattn_ln_beta, L0_xattn_residual_scale)
    x = x + _L0_attn_ref(_layernorm(x, axis=-1), L0_attn_w_qa, L0_attn_q_a_ln_w, L0_attn_w_qb, L0_attn_w_kva, L0_attn_kv_a_ln_w, L0_attn_w_kvb, L0_attn_w_o)
    x = x + _L0_ffn_ref(_layernorm(x, axis=-1), L0_ffn_gate_weight, L0_ffn_gate_up_proj, L0_ffn_down_proj, L0_ffn_old_to_new)
    return x

_drawn_inputs = setup_inputs


def setup_inputs(seed=0):
    import zlib

    import numpy as np

    out = dict(_drawn_inputs(seed))
    spreads = {'L0_xattn_bq': (0.0, 0.316),
     'L0_xattn_bk': (0.0, 0.8),
     'L0_xattn_bv': (0.0, 0.1),
     'L0_xattn_bo': (0.0, 0.1),
     'L0_xattn_ln_gamma': (1.0, 0.2),
     'L0_xattn_ln_beta': (0.0, 0.1),
     'L0_attn_q_a_ln_w': (1.0, 0.6),
     'L0_attn_kv_a_ln_w': (1.0, 0.2)}
    factors = {'L0_ffn_gate_weight': 7.562, 'L0_ffn_gate_up_proj': 6.042, 'L0_ffn_down_proj': 6.036}
    for name, (base, spread) in spreads.items():
        noise = np.random.default_rng([zlib.crc32(name.encode()), seed]).standard_normal(out[name].shape)
        drawn = base * np.exp(spread * noise) if base else spread * noise
        out[name] = jnp.asarray(drawn.astype(out[name].dtype))
    for name, factor in factors.items():
        out[name] = (out[name] * factor).astype(out[name].dtype)
    return out
```

```python
import concourse.bass as bass
from concourse import mybir
from contextlib import ExitStack
import numpy as np


T, HID = 256, 512
TT, HC = T // 128, HID // 128
S2 = 4096
XH, XD = 16, 32
CB = 512
NBLK, CT = S2 // CB, CB // 128
STEPS = CT * HC
QLR, KVLR, DN, DR, DV = 384, 128, 128, 64, 128
MH = 16
PAIRS = MH // 2
QC = QLR // 128
NEXP, KEPT, TOPK, INTER, CAP = 128, 48, 8, 192, 192
UNITS = KEPT * INTER // 128
UNROLL = 6
UW = HC * 256 + HID
SA, SW, SH = 64.0, 256.0, 16.0
NEG = -1.0e30
MLA_SCALE = float(DN + DR) ** -0.5
X_SCALE = float(XD) ** -0.5


def build(nc, a, out):
    f32, f16, i32 = mybir.dt.float32, mybir.dt.float16, mybir.dt.int32
    ALU, ACT, AX = mybir.AluOpType, mybir.ActivationFunctionType, mybir.AxisListType

    ctx = ExitStack()
    with ctx:
        def sb(name, shape, dt=f32):
            return ctx.enter_context(nc.sbuf_tensor(name, shape, dt))

        def sem(name):
            return ctx.enter_context(nc.semaphore(name))

        pS = ctx.enter_context(nc.psum_tensor("pS", [128, 4, 512], f32))
        pO = ctx.enter_context(nc.psum_tensor("pO", [128, 2, 512], f32))
        pD = ctx.enter_context(nc.psum_tensor("pD", [128, 512], f32))
        pP = ctx.enter_context(nc.psum_tensor("pP", [128, 512], f32))

        def step_scores(st):
            return pS[:, 2 * (st % 2):2 * (st % 2) + 2, :].rearrange("p b (h q) -> p (b h) q", h=2)

        x_sb = sb("x_sb", [128, TT, HID])
        x1_sb = sb("x1_sb", [128, TT, HID])
        xn = sb("xn", [128, TT, HID])
        xT = sb("xT", [128, HC, T])
        work = sb("work", [128, 2, HID])
        bo_b = sb("bo_b", [128, HID])
        gam_b = sb("gam_b", [128, HID])
        bet_b = sb("bet_b", [128, HID])
        woT = sb("woT", [128, HC, HID])
        gateT = sb("gateT", [128, HC, NEXP])
        wqaT = sb("wqaT", [128, HC, QLR])
        wkvaT = sb("wkvaT", [128, HC, KVLR + 256])
        cosT = sb("cosT", [128, T])
        sinT = sb("sinT", [128, T])
        xb = sb("xb", [128, 3, HC])
        lnw = sb("lnw", [128, QC + 1])
        rs = sb("rs", [128, 1])
        mask_i = sb("mask_i", [128, S2 // 128], i32)
        mtab = sb("mtab", [128, NBLK, 2, CT])
        mblk = sb("mblk", [128, 2, 2, CT])
        o2n_c = sb("o2n_c", [128, 1], i32)
        o2n_r = sb("o2n_r", [128, NEXP], i32)
        ident = sb("ident", [128, 128])
        ones = sb("ones", [128, 128])
        tri = sb("tri", [128, 128])
        cmask = sb("cmask", [128, 128])
        zero16 = sb("zero16", [128, 512], f16)
        onecol = sb("onecol", [128, HC, 32])
        selrow = sb("selrow", [128, HC, 128])
        iota_i = sb("iota_i", [128, KEPT], i32)
        nhalf = sb("nhalf", [128, 2])
        bn = sb("bn", [128, TT, 6])
        mv = sb("mv", [128, TT, 2])
        var = sb("var", [128, TT])
        rstd = sb("rstd", [128, TT])
        mw_in = sb("mw_in", [128, 2, QC * 512 + 512])
        mw_out = sb("mw_out", [128, 2, 1024])

        ARENA = 31744
        arena = sb("arena", [128, ARENA])
        at = [0]

        def take(n, dt=f32):
            words = n if dt == f32 else n // 2
            v = arena[:, at[0]:at[0] + words]
            at[0] += words
            assert at[0] <= ARENA
            return v if dt == f32 else v.bitcast(dt)

        cbuf = take(2 * HC * CB).rearrange("p (b c t) -> p b c t", b=2, c=HC)
        chi = take(2 * HC * CB, f16).rearrange("p (b c t) -> p b c t", b=2, c=HC)
        clo = take(2 * HC * CB, f16).rearrange("p (b c t) -> p b c t", b=2, c=HC)
        wk16 = take(2 * HC * HID, f16).rearrange("p (s c n) -> p s c n", s=2, c=HC)
        wv16 = take(2 * HC * HID, f16).rearrange("p (s c n) -> p s c n", s=2, c=HC)
        kh = take(HC * CB, f16).rearrange("p (g t) -> p g t", g=HC)
        kl = take(HC * CB, f16).rearrange("p (g t) -> p g t", g=HC)
        kf = take(2 * CB).rearrange("p (b t) -> p b t", b=2)
        v_sb = take(2 * CT * HID).rearrange("p (b t n) -> p b t n", b=2, t=CT)
        wqT = v_sb[:, 1]
        q_st = take(XH * T, f16).rearrange("p (j g q) -> p j g q", j=4, g=HC)
        probs = take(2 * 4 * T).rearrange("p (b j q) -> p b j q", b=2, j=4)
        k_at = at[0]
        k_st = take(2 * XH * CB, f16).rearrange("p (b j g t) -> p b j g t", b=2, j=4, g=HC)
        wk32 = arena[:, k_at + 4096:k_at + 6144].rearrange("p (c n) -> p c n", c=HC)
        wv32 = arena[:, k_at + 6144:k_at + 8192].rearrange("p (c n) -> p c n", c=HC)
        qh, ql = kh[:, :, 0:T], kl[:, :, 0:T]
        x_end = at[0]
        at[0] = 0
        uw32 = take(UNROLL * UW).rearrange("p (b n) -> p b n", b=UNROLL)
        uwh = take(3 * UW, f16).rearrange("p (b n) -> p b n", b=3)
        uwl = take(3 * UW, f16).rearrange("p (b n) -> p b n", b=3)
        wb = take(UNROLL * T).rearrange("p (b t) -> p b t", b=UNROLL)
        xh = take(HC * T, f16).rearrange("p (c t) -> p c t", c=HC)
        xl = take(HC * T, f16).rearrange("p (c t) -> p c t", c=HC)
        sg = take(2 * T).rearrange("p (b t) -> p b t", b=2)
        m1 = take(2 * T).rearrange("p (b t) -> p b t", b=2)
        m2 = take(2 * T).rearrange("p (b t) -> p b t", b=2)
        hh = take(2 * T, f16).rearrange("p (b t) -> p b t", b=2)
        hl = take(2 * T, f16).rearrange("p (b t) -> p b t", b=2)
        ctxn = take(HC * T).rearrange("p (g q) -> p g q", g=HC)
        rden = take(HC * T).rearrange("p (g q) -> p g q", g=HC)
        den = take(T)
        cqn = take(TT * QLR).rearrange("p (t n) -> p t n", t=TT)
        kvn = take(TT * KVLR).rearrange("p (t n) -> p t n", t=TT)
        ssq = take(2 * TT)
        lrs = take(2 * TT)
        lat = take((QC + 1) * T).rearrange("p (c t) -> p c t", c=QC + 1)
        kpe = take(T)
        rp1 = take(T)
        rp2 = take(T)
        qn = take(4 * T).rearrange("p (b j t) -> p b j t", b=2, j=2)
        kn = take(4 * T).rearrange("p (b j t) -> p b j t", b=2, j=2)
        vv = take(4 * T).rearrange("p (b t n) -> p b t n", b=2, t=TT)
        qpe = take(2 * T).rearrange("p (b t) -> p b t", b=2)
        pm = take(2 * 384).rearrange("p (j k) -> p j k", j=2)
        pt = take(2 * 384).rearrange("p (j k) -> p j k", j=2)
        aT = take(2 * T).rearrange("p (j t) -> p j t", j=2)
        mx = take(4).rearrange("p (t j) -> p t j", t=2)
        nm = take(4).rearrange("p (t j) -> p t j", t=2)
        sm = take(4).rearrange("p (t j) -> p t j", t=2)
        rc = take(4).rearrange("p (t j) -> p t j", t=2)
        keep = take(NEXP)
        nkeep = take(NEXP)
        o2n_f = take(NEXP)
        o2n_cf = take(1)
        iota_f = take(KEPT)
        emap = take(KEPT)
        lm = take(TT * NEXP).rearrange("p (t n) -> p t n", t=TT)
        rep = take(TT * NEXP).rearrange("p (t n) -> p t n", t=TT)
        sel = take(TT * NEXP).rearrange("p (t n) -> p t n", t=TT)
        ex = take(TT * NEXP).rearrange("p (t n) -> p t n", t=TT)
        top = take(TT * TOPK).rearrange("p (t n) -> p t n", t=TT)
        ntop = take(TT)
        zs = take(TT)
        zr = take(TT)
        wT = take(T)
        wnew = take(T)
        assert x_end <= ARENA

        wdram = nc.dram_tensor("w_scratch", [KEPT, T], f32, kind="Internal").ap()

        names = """x_in small_in row_in wq_in wkv_in wo_in gate_in qa_in kva_in rope_in
            var_ready rstd_ready xn_ready tr_done xT_ready
            const_ready zc_ready prep_ready wk_hi wk_lo q_mm q_f q_hi q_lo q_stacked
            ctx_hi ctx_lo proj_done proj_evac k_f k_hi k_lo k_stacked
            scores_done exp_done clip_done pv_done acc_zero
            x_acc_done den_ready denb_done ctxn_ready delta_done x1_ready
            lat_mm ssq_ready lvar_ready lrstd_ready latn_ready lat_tr lat_ready kpe_ready rope_step
            mproj_done qkv_ready rope_ready s_done masked maxed negmax exps_done rec_ready p_ready
            pt_done pt_ready o_done o_ready wo_done mla_done x2_ready
            xh_ready xl_ready logits_done lm_ready top_ready rep_ready ntop_ready ex_ready sel_ready
            cnt_done w_ready wt_done wt_ready wn_done wn_ready w_stored
            unit_hi unit_lo gu_done silu_ready m1_ready m2_ready h_hi h_lo down_done moe_done
            out_ready out_stored dch pch ach""".split()
        s = {n: sem(n) for n in names}
        ctx_in = [sem(f"ctx_in{i}") for i in range(2)]
        mblk_in = [sem(f"mblk_in{i}") for i in range(2)]
        min_in = [sem(f"mla_in{i}") for i in range(2)]
        mout_in = [sem(f"mla_out_in{i}") for i in range(2)]
        unit_in = [sem(f"unit_in{i}") for i in range(UNROLL)]
        wb_in = [sem(f"wb_in{i}") for i in range(UNROLL)]

        STACK_DMAS = 16
        block = ctx.enter_context(nc.Block())

        @block.sync
        def _(sp):
            def load_ctx(b, p):
                sp.dma_start(cbuf[:, p], a["ctxT"][b]).then_inc(ctx_in[p], 16)

            def load_mask(b, p):
                sp.dma_start(mblk[:, p], mtab[:, b]).then_inc(mblk_in[p], 16)

            def stack_k(b, p):
                sp.wait_ge(s["k_lo"], 4 * (b + 1))
                for j in range(4):
                    for part, src in ((0, kh), (1, kl), (2, kh), (3, kl)):
                        sp.dma_start(k_st[32 * part:32 * part + 32, p, j], src[32 * j:32 * j + 32, :, :])\
                          .then_inc(s["k_stacked"], 16)

            def load_mla_in(m, p):
                sp.dma_start(mw_in[:, p], a["mla_in"][m]).then_inc(min_in[p], 16)

            def load_mla_out(m, p):
                sp.dma_start(mw_out[:, p], a["mla_out"][m]).then_inc(mout_in[p], 16)

            def load_unit(n, slot):
                sp.dma_start(uw32[:, slot], a["units"][n]).then_inc(unit_in[slot], 16)

            def load_wb(it, slot):
                pair = 2 * it + slot // 3
                for half in range(2):
                    e = 2 * pair + (half if slot % 3 == 2 else slot % 3)
                    sp.dma_start(wb[64 * half:64 * half + 64, slot],
                                 wdram[e, :].unsqueeze(0).broadcast_to([64, T])
                                 ).then_inc(wb_in[slot], 16)

            sp.dma_start(x_sb[:, :, :], a["x"]).then_inc(s["x_in"], 16)
            load_ctx(0, 0)
            sp.dma_start(wk32, a["wkT"]).then_inc(s["wkv_in"], 16)
            sp.dma_start(wv32, a["wvT"]).then_inc(s["wkv_in"], 16)
            sp.dma_start(wqT[:, :, :], a["wqT"]).then_inc(s["wq_in"], 16)
            load_ctx(1, 1)
            sp.dma_start(woT[:, :, :], a["woT"]).then_inc(s["wo_in"], 16)
            sp.dma_start(wqaT[:, :, :], a["wqaT"]).then_inc(s["qa_in"], 16)
            sp.dma_start(wkvaT[:, :, :], a["wkvaT"]).then_inc(s["kva_in"], 16)
            sp.dma_start(cosT[:, :], a["cosT"]).then_inc(s["rope_in"], 16)
            sp.dma_start(sinT[:, :], a["sinT"]).then_inc(s["rope_in"], 16)
            sp.dma_start(gateT[:, :, :], a["gateT"]).then_inc(s["gate_in"], 16)
            for m in range(2):
                load_mla_in(m, m)
                load_mla_out(m, m)
            sp.wait_ge(s["q_lo"], 1)
            for j in range(4):
                for part, src in ((0, qh), (1, qh), (2, ql), (3, ql)):
                    sp.dma_start(q_st[32 * part:32 * part + 32, j], src[32 * j:32 * j + 32]).then_inc(s["q_stacked"], 16)
            sp.wait_ge(s["prep_ready"], 1)
            load_mask(0, 0)
            stack_k(0, 0)

            def x_block(b, p, stack=True, load=True):
                if load:
                    sp.wait_ge(s["ctx_lo"], 4 * (b + 1))
                    sp.nop()
                    load_ctx(b + 2, p)
                if stack:
                    sp.wait_ge(s["exp_done"], STEPS * b + 1)
                    sp.nop()
                    load_mask(b + 1, 1 - p)
                    stack_k(b + 1, 1 - p)

            with sp.Fori(0, NBLK - 3, 2) as b:
                x_block(b, 0)
                x_block(b + 1, 1)
            x_block(NBLK - 2, 0, load=False)

            sp.wait_ge(s["x_acc_done"], 1)
            for n in range(UNROLL):
                load_unit(n, n)

            with sp.Fori(0, PAIRS - 3, 2) as m:
                for p in range(2):
                    sp.wait_ge(s["mproj_done"], 4 * (m + p + 1))
                    sp.nop()
                    load_mla_in(m + p + 2, p)
                    sp.wait_ge(s["wo_done"], m + p + 1)
                    sp.nop()
                    load_mla_out(m + p + 2, p)

            sp.wait_ge(s["wn_ready"], 1)
            sp.dma_start(wdram, wnew[0:KEPT, :]).then_inc(s["w_stored"], 16)
            sp.wait_ge(s["w_stored"], 16)
            for slot in range(UNROLL):
                load_wb(0, slot)
            with sp.Fori(0, UNITS // UNROLL - 1) as it:
                for slot in range(UNROLL):
                    n = UNROLL * it + slot
                    sp.wait_ge(s["unit_lo"], n + 1)
                    sp.nop()
                    load_unit(n + UNROLL, slot)
                    sp.wait_ge(s["m2_ready"], n + 1)
                    sp.nop()
                    load_wb(it + 1, slot)

            sp.wait_ge(s["out_ready"], 1)
            sp.dma_start(out, work[:, :, :]).then_inc(s["out_stored"], 16)
            sp.wait_ge(s["out_stored"], 16)

        @block.gpsimd
        def _(pool):
            chain = [0]

            def link(ins):
                chain[0] += 1
                ins.then_inc(s["pch"], 1)
                pool.wait_ge(s["pch"], chain[0])

            for dst, src in ((xb[:, :, :], a["xb"]), (lnw[:, :], a["lnw"]), (mask_i[:, :], a["mask"]),
                             (rs[:, :], a["rs"].broadcast_to([128, 1])), (o2n_c[:, :], a["o2n_c"]),
                             (o2n_r[:, :], a["o2n_r"].broadcast_to([128, NEXP]))):
                pool.dma_start(dst, src).then_inc(s["small_in"], 16)
            for dst, src in ((bo_b, "bo"), (gam_b, "gamma"), (bet_b, "beta")):
                pool.dma_start(dst[:, :], a[src].broadcast_to([128, HID])).then_inc(s["row_in"], 16)
            pool.memset(nhalf[:, :], -0.5).then_inc(s["pch"], 1)
            pool.memset(ident[:, :], 0.0).then_inc(s["pch"], 1)
            pool.memset(zero16[:, :], 0.0).then_inc(s["pch"], 1)
            pool.memset(onecol[:, :, :], 0.0).then_inc(s["pch"], 1)
            pool.memset(selrow[:, :, :], 0.0).then_inc(s["pch"], 1)
            pool.memset(ones[:, :], 1.0).then_inc(s["pch"], 1)
            pool.memset(tri[:, :], 1.0).then_inc(s["pch"], 1)
            chain[0] = 7
            link(pool.memset(cmask[:, :], 0.0))
            link(pool.affine_select(out=ident[:, :], in_=ident[:, :], compare_op=ALU.not_equal, fill=1.0, base=0,
                                    pattern=[[-1, 128]], channel_multiplier=1))
            for g in range(HC):
                link(pool.memset(onecol[:, g, g:g + 1], 1.0))
            pool.nop().then_inc(s["const_ready"], 1)

            pool.wait_ge(s["var_ready"], 1)
            pool.tensor_tensor(rstd[:, :], var[:, :], nhalf[:, :], ALU.pow).then_inc(s["rstd_ready"], 1)

            link(pool.affine_select(out=selrow[:, :, :].rearrange("p g (j m) -> p g j m", j=4),
                                    in_=selrow[:, :, :].rearrange("p g (j m) -> p g j m", j=4),
                                    compare_op=ALU.not_equal, fill=1.0, base=0,
                                    pattern=[[-1, HC], [-32, 4], [0, 32]], channel_multiplier=1))
            link(pool.affine_select(out=tri[:, :], in_=tri[:, :], compare_op=ALU.is_ge, fill=0.0, base=0,
                                    pattern=[[1, 128]], channel_multiplier=-1))
            link(pool.affine_select(out=cmask[:, :], in_=cmask[:, :], compare_op=ALU.is_ge, fill=NEG, base=0,
                                    pattern=[[-1, 128]], channel_multiplier=1))
            link(pool.iota(iota_i[:, :], pattern=[[1, KEPT]], base=0, channel_multiplier=0))
            pool.nop().then_inc(s["zc_ready"], 1)
            pool.wait_ge(s["var_ready"], 2)
            pool.tensor_tensor(rstd[:, :], var[:, :], nhalf[:, :], ALU.pow).then_inc(s["rstd_ready"], 1)
            pool.wait_ge(s["var_ready"], 3)
            pool.tensor_tensor(rstd[:, :], var[:, :], nhalf[:, :], ALU.pow).then_inc(s["rstd_ready"], 1)
            pool.wait_ge(s["lvar_ready"], 1)
            for i in range(2):
                last = pool.tensor_tensor(lrs[:, TT * i:TT * i + TT], ssq[:, TT * i:TT * i + TT], nhalf[:, :], ALU.pow)
            last.then_inc(s["lrstd_ready"], 1)
            pool.wait_ge(s["var_ready"], 4)
            pool.tensor_tensor(rstd[:, :], var[:, :], nhalf[:, :], ALU.pow).then_inc(s["rstd_ready"], 1)

        @block.scalar
        def _(act):
            def transposed(k):
                act.wait_ge(s["tr_done"], k)
                for i in range(2):
                    last = act.activation(xT[:, 2 * i:2 * i + 2, :], pS[:, i, :].rearrange("p (c t) -> p c t", c=2), ACT.Copy)
                last.then_inc(s["xT_ready"], 1)

            def split_ctx(p, c, b=0):
                act.activation(chi[:, p, c], cbuf[:, p, c], ACT.Copy, scale=SA).then_inc(s["ctx_hi"], 1)

            act.wait_ge(s["wkv_in"], 32)
            for c in range(HC):
                act.activation(wk16[:, 0, c], wk32[:, c], ACT.Copy, scale=SW)
                last = act.activation(wv16[:, 0, c], wv32[:, c], ACT.Copy, scale=SW)
            last.then_inc(s["wk_hi"], 1)
            act.wait_ge(ctx_in[0], 16)
            for c in range(HC):
                split_ctx(0, c)
            transposed(1)
            act.wait_ge(s["q_mm"], 1)
            act.wait_ge(s["prep_ready"], 1)
            for g in range(HC):
                last = act.activation(q_f32(probs, g), pS[:, 2 + g // 2, 256 * (g % 2):256 * (g % 2) + 256],
                                      ACT.Identity, bias=xb[:, 0, g:g + 1], scale=SA)
            last.then_inc(s["q_f"], 1)
            act.wait_ge(ctx_in[1], 16)
            for c in range(HC):
                split_ctx(1, c)

            def evac(b, p, n, first=False):
                act.wait_ge(s["proj_done"], 8 * b + n + 1)
                if n < HC:
                    if not (first and n < 2):
                        act.wait_ge(s["k_lo"], 4 * b + n - 1)
                    act.activation(kf[:, n % 2], pP[:, :], ACT.Identity, bias=xb[:, 1, n:n + 1],
                                   scale=1.0 / SW).then_inc(s["proj_evac"], 1)
                else:
                    act.activation(v_sb[:, p, n - HC], pP[:, :], ACT.Copy,
                                   scale=1.0 / (SA * SW)).then_inc(s["proj_evac"], 1)

            act.wait_ge(s["q_lo"], 1)
            for n in range(8):
                evac(0, 0, n, first=True)

            def x_block(b, p, proj=True, split=True):
                for st in range(STEPS):
                    if proj and st % 2:
                        evac(b + 1, 1 - p, st // 2)
                    act.wait_ge(s["scores_done"], STEPS * b + st + 1)
                    if st == 0:
                        act.wait_ge(mblk_in[p], 16 * (b // 2 + 1) if isinstance(b, int) else 8 * (b - p) + 16)
                    act.activation(probs[:, st % 2], step_scores(st), ACT.Exp,
                                   bias=mblk[:, p, 1, st // HC:st // HC + 1], scale=mblk[:, p, 0, st // HC:st // HC + 1])\
                       .then_inc(s["exp_done"], 1)
                    if split and st % 2 == 0 and st >= 8:
                        if st == 8:
                            act.wait_ge(ctx_in[p], 8 * b + 32 if isinstance(b, int) else (b - p) * 8 + 32)
                            act.wait_ge(s["proj_done"], 8 * (b + 1))
                        split_ctx(p, (st - 8) // 2)

            with act.Fori(0, NBLK - 3, 2) as b:
                x_block(b, 0)
                x_block(b + 1, 1)
            x_block(NBLK - 2, 0, split=False)
            x_block(NBLK - 1, 1, proj=False, split=False)

            transposed(2)
            act.wait_ge(s["lat_mm"], 1)
            for t in range(TT):
                act.activation(work[:, 0, 0:QLR], pS[:, 2 + t, 0:QLR], ACT.Square, accum_out=ssq[:, t:t + 1]).then_inc(s["ach"], 1)
                act.wait_ge(s["ach"], 2 * t + 1)
                act.activation(work[:, 0, 0:KVLR], pO[:, 0, KVLR * t:KVLR * t + KVLR], ACT.Square,
                               accum_out=ssq[:, TT + t:TT + t + 1]).then_inc(s["ach"], 1)
                act.wait_ge(s["ach"], 2 * t + 2)
            act.nop().then_inc(s["ssq_ready"], 1)

            def mla_evac(m, p):
                for n, (dst, src) in enumerate(((qn[:, p], pS[:, 0, :]), (kn[:, p], pS[:, 2, :]), (vv[:, p], pS[:, 3, :]))):
                    act.wait_ge(s["mproj_done"], 4 * m + (1, 3, 4)[n])
                    act.activation(dst, src.rearrange("p (j t) -> p j t", j=2), ACT.Copy).then_inc(s["qkv_ready"], 1)

            def mla_exps(m):
                act.wait_ge(s["negmax"], m + 1)
                for j in range(2):
                    for t, (lo, hi) in enumerate(((0, 128), (128, 384))):
                        last = act.activation(pm[:, j, lo:hi], pO[:, j, lo:hi], ACT.Exp, bias=nm[:, t, j:j + 1],
                                              scale=MLA_SCALE, accum_out=sm[:, t, j:j + 1])
                last.then_inc(s["exps_done"], 1)

            def mla_pair(m, p, proj=True):
                mla_exps(m)
                if proj:
                    mla_evac_q(m + 1, 1 - p)
                act.wait_ge(s["pt_done"], m + 1)
                act.activation(pt, pO[:, :, 0:384], ACT.Copy).then_inc(s["pt_ready"], 1)
                if proj:
                    mla_evac_kv(m + 1, 1 - p)

            def mla_evac_q(m, p):
                act.wait_ge(s["mproj_done"], 4 * m + 1)
                act.activation(qn[:, p], pS[:, 0, :].rearrange("p (j t) -> p j t", j=2), ACT.Copy).then_inc(s["qkv_ready"], 1)

            def mla_evac_kv(m, p):
                act.wait_ge(s["mproj_done"], 4 * m + 3)
                act.activation(kn[:, p], pS[:, 2, :].rearrange("p (j t) -> p j t", j=2), ACT.Copy).then_inc(s["qkv_ready"], 1)
                act.wait_ge(s["mproj_done"], 4 * m + 4)
                act.activation(vv[:, p], pS[:, 3, :].rearrange("p (j t) -> p j t", j=2), ACT.Copy).then_inc(s["qkv_ready"], 1)

            mla_evac_q(0, 0)
            mla_evac_kv(0, 0)
            with act.Fori(0, PAIRS - 3, 2) as m:
                mla_pair(m, 0)
                mla_pair(m + 1, 1)
            mla_pair(PAIRS - 2, 0)
            mla_pair(PAIRS - 1, 1, proj=False)

            def split_unit(n, slot, ring):
                act.activation(uwh[:, ring], uw32[:, slot], ACT.Copy, scale=SW).then_inc(s["unit_hi"], 1)

            def hidden(n, bank, buf):
                act.wait_ge(s["gu_done"], n + 1)
                act.activation(sg[:, buf], pS[:, bank, 0:T], ACT.Silu, scale=1.0 / (SA * SW)).then_inc(s["silu_ready"], 1)
                act.wait_ge(s["m2_ready"], n + 1)
                act.activation(hh[:, buf], m2[:, buf], ACT.Copy).then_inc(s["h_hi"], 1)

            transposed(3)
            act.wait_ge(s["ntop_ready"], 1)
            for t in range(TT):
                last = act.activation(ex[:, t], lm[:, t], ACT.Exp, bias=ntop[:, t:t + 1])
            last.then_inc(s["ex_ready"], 1)
            for c in range(HC):
                last = act.activation(xh[:, c], xT[:, c, :], ACT.Copy, scale=SA)
            last.then_inc(s["xh_ready"], 1)
            for n in range(2):
                act.wait_ge(unit_in[n], 16)
                split_unit(n, n, n)
            hidden(0, 0, 0)

            def moe_units(it, last_turn=False):
                for u in range(UNROLL):
                    n = UNROLL * it + u
                    if not (last_turn and u + 2 >= UNROLL):
                        slot = (u + 2) % UNROLL
                        act.wait_ge(unit_in[slot], 16 * (it + 1 + (u + 2) // UNROLL))
                        act.wait_ge(s["down_done"], n + 1)
                        split_unit(n + 2, slot, (u + 2) % 3)
                    if not (last_turn and u + 1 >= UNROLL):
                        hidden(n + 1, (u + 1) % 3, (u + 1) % 2)

            with act.Fori(0, UNITS // UNROLL - 1) as it:
                moe_units(it)
            moe_units(UNITS // UNROLL - 1, last_turn=True)

        @block.vector
        def _(dve):
            chain = [0]

            def link(ins):
                chain[0] += 1
                ins.then_inc(s["dch"], 1)
                dve.wait_ge(s["dch"], chain[0])

            def norm_stats(src, k, eps):
                for t in range(TT):
                    link(dve.bn_stats(bn[:, t, :], src[:, t, :]))
                    link(dve.bn_aggr(mv[:, t, :], bn[:, t, :]))
                dve.tensor_scalar(var[:, :], mv[:, :, 1], eps, None, ALU.add).then_inc(s["var_ready"], 1)
                dve.wait_ge(s["rstd_ready"], k)

            def norm(src, dst, k, eps=1e-5):
                norm_stats(src, k, eps)
                for t in range(TT):
                    last = dve.tensor_scalar(dst[:, t, :], src[:, t, :], mv[:, t, 0:1], rstd[:, t:t + 1],
                                             ALU.subtract, ALU.mult)
                return last

            dve.wait_ge(s["x_in"], 16)
            norm(x_sb, xn, 1).then_inc(s["xn_ready"], 1)
            dve.wait_ge(s["small_in"], 16 * 6)
            link(dve.tensor_scalar(xb[:, 0:2, :], xb[:, 0:2, :], SA, None, ALU.mult))
            mview = mask_i[:, :].rearrange("p (b t) -> p b t", t=CT)
            dve.tensor_scalar(mtab[:, :, 0, :], mview, 0.5, X_SCALE / (SA * SA), ALU.is_gt, ALU.mult)
            link(dve.tensor_scalar(mtab[:, :, 1, :], mview, 0.5, None, ALU.is_gt))
            link(dve.tensor_scalar(mtab[:, :, 1, :], mtab[:, :, 1, :], 1.0, 50.0, ALU.subtract, ALU.mult))
            link(dve.tensor_scalar(rs[:, :], rs[:, :], 0.0, 0.3, ALU.max, ALU.min))
            dve.nop().then_inc(s["prep_ready"], 1)
            dve.wait_ge(s["wk_hi"], 1)
            for c in range(HC):
                dve.scalar_tensor_tensor(wk16[:, 1, c], wk32[:, c], SW, wk16[:, 0, c], ALU.mult, ALU.subtract)
                last = dve.scalar_tensor_tensor(wv16[:, 1, c], wv32[:, c], SW, wv16[:, 0, c], ALU.mult, ALU.subtract)
            last.then_inc(s["wk_lo"], 1)

            def split_ctx(b, p, c):
                dve.wait_ge(s["ctx_hi"], 4 * b + c + 1)
                dve.scalar_tensor_tensor(clo[:, p, c], cbuf[:, p, c], SA, chi[:, p, c],
                                         ALU.mult, ALU.subtract).then_inc(s["ctx_lo"], 1)

            for c in range(HC):
                split_ctx(0, 0, c)
            dve.wait_ge(s["q_f"], 1)
            for g in range(HC):
                dve.tensor_copy(qh[:, g], q_f32(probs, g)).then_inc(s["q_hi"], 1)
            for g in range(HC):
                dve.wait_ge(s["q_hi"], g + 1)
                last = dve.tensor_tensor(ql[:, g], q_f32(probs, g), qh[:, g], ALU.subtract)
            last.then_inc(s["q_lo"], 1)
            for c in range(HC):
                split_ctx(1, 1, c)

            def split_k(b, n, first=False):
                if n == 0:
                    if first:
                        dve.wait_ge(s["q_stacked"], 16 * 16)
                    else:
                        dve.wait_ge(s["k_stacked"], 16 * STACK_DMAS * b)
                dve.wait_ge(s["proj_evac"], 8 * b + n + 1)
                dve.tensor_copy(kh[:, n], kf[:, n % 2]).then_inc(s["k_hi"], 1)
                dve.wait_ge(s["k_hi"], 4 * b + n + 1)
                dve.tensor_tensor(kl[:, n], kf[:, n % 2], kh[:, n], ALU.subtract).then_inc(s["k_lo"], 1)

            for n in range(HC):
                split_k(0, n, first=True)

            LO, HI = float(np.exp(np.float32(-50.0))), float(np.exp(np.float32(50.0)))

            def x_block(b, p, proj=True, split=True):
                for st in range(STEPS):
                    if proj and st % 2 and st // 2 < HC:
                        split_k(b + 1, st // 2)
                    dve.wait_ge(s["exp_done"], STEPS * b + st + 1)
                    dve.tensor_scalar(probs[:, st % 2], probs[:, st % 2], LO, HI, ALU.max, ALU.min)\
                       .then_inc(s["clip_done"], 1)
                    if split and st % 2 == 0 and st >= 8:
                        if st == 8:
                            dve.wait_ge(s["proj_done"], 8 * (b + 1))
                        split_ctx(b + 2, p, (st - 8) // 2)

            with dve.Fori(0, NBLK - 3, 2) as b:
                x_block(b, 0)
                x_block(b + 1, 1)
            x_block(NBLK - 2, 0, split=False)
            x_block(NBLK - 1, 1, proj=False, split=False)

            dve.wait_ge(s["x_acc_done"], 1)
            dve.tensor_copy(den, pD[:, 0:T]).then_inc(s["den_ready"], 1)
            dve.wait_ge(s["denb_done"], 1)
            for i in range(2):
                link(dve.reciprocal(rden[:, 2 * i:2 * i + 2, :], pS[:, i, :].rearrange("p (g q) -> p g q", g=2)))
                link(dve.tensor_tensor(ctxn[:, 2 * i:2 * i + 2, :], pO[:, i, :].rearrange("p (g q) -> p g q", g=2),
                                       rden[:, 2 * i:2 * i + 2, :], ALU.mult))
            for g in range(HC):
                last = dve.tensor_scalar(ctxn[:, g], ctxn[:, g], xb[:, 2, g:g + 1], None, ALU.add)
            last.then_inc(s["ctxn_ready"], 1)
            dve.wait_ge(s["delta_done"], 1)
            dve.wait_ge(s["row_in"], 48)
            for t in range(TT):
                link(dve.tensor_tensor(work[:, t, :], pS[:, 2 + t, :], bo_b[:, :], ALU.add))
                link(dve.tensor_scalar(work[:, t, :], work[:, t, :], rs[:, 0:1], None, ALU.mult))
            link(norm(work, work, 2))
            for t in range(TT):
                link(dve.tensor_tensor(work[:, t, :], work[:, t, :], gam_b[:, :], ALU.mult))
                link(dve.tensor_tensor(work[:, t, :], work[:, t, :], bet_b[:, :], ALU.add))
                link(dve.tensor_tensor(x1_sb[:, t, :], work[:, t, :], x_sb[:, t, :], ALU.add))

            norm(x1_sb, xn, 3).then_inc(s["xn_ready"], 1)
            dve.wait_ge(s["ssq_ready"], 1)
            link(dve.tensor_scalar(ssq[:, 0:TT], ssq[:, 0:TT], 1.0 / QLR, 1e-6, ALU.mult, ALU.add))
            dve.tensor_scalar(ssq[:, TT:2 * TT], ssq[:, TT:2 * TT], 1.0 / KVLR, 1e-6, ALU.mult, ALU.add)\
               .then_inc(s["lvar_ready"], 1)
            dve.wait_ge(s["lrstd_ready"], 1)
            for t in range(TT):
                dve.tensor_scalar(cqn[:, t], pS[:, 2 + t, 0:QLR], lrs[:, t:t + 1], None, ALU.mult)
                last = dve.tensor_scalar(kvn[:, t], pO[:, 0, KVLR * t:KVLR * t + KVLR], lrs[:, TT + t:TT + t + 1], None, ALU.mult)
            last.then_inc(s["latn_ready"], 1)
            dve.wait_ge(s["rope_in"], 32)
            link(dve.tensor_tensor(rp1, pO[:, 1, 0:T], cosT[:, :], ALU.mult))
            link(dve.tensor_tensor(rp2, pO[:, 1, T:2 * T], sinT[:, :], ALU.mult))
            link(dve.tensor_tensor(kpe, rp1, rp2, ALU.add))
            dve.nop().then_inc(s["kpe_ready"], 1)
            dve.wait_ge(s["lat_tr"], 1)
            for c in range(QC + 1):
                last = dve.tensor_scalar(lat[:, c], pS[:, c // 2, 256 * (c % 2):256 * (c % 2) + 256], lnw[:, c:c + 1], None, ALU.mult)
            last.then_inc(s["lat_ready"], 1)

            def rope_q(m, p):
                dve.wait_ge(s["mproj_done"], 4 * m + 2)
                dve.tensor_tensor(rp1, pS[:, 1, 0:T], cosT[:, :], ALU.mult).then_inc(s["rope_step"], 1)
                dve.tensor_tensor(rp2, pS[:, 1, T:2 * T], sinT[:, :], ALU.mult).then_inc(s["rope_step"], 1)
                dve.wait_ge(s["rope_step"], 2 * m + 2)
                dve.tensor_tensor(qpe[:, p], rp1, rp2, ALU.add).then_inc(s["rope_ready"], 1)

            diag = pO[:, :, 0:384].rearrange("p j (b k) -> p j b k", k=128)

            def mla_pair(m, p, proj=True):
                dve.wait_ge(s["s_done"], m + 1)
                for j in range(2):
                    last = dve.tensor_tensor(diag[:, j, 0:3:2, :], diag[:, j, 0:3:2, :],
                                             cmask[:, :].unsqueeze(1).broadcast_to([128, 2, 128]), ALU.add)
                last.then_inc(s["masked"], 1)
                dve.wait_ge(s["masked"], m + 1)
                dve.reduce_max(mx[:, 0, :], pO[:, :, 0:128], AX.X)
                dve.reduce_max(mx[:, 1, :], pO[:, :, 128:384], AX.X).then_inc(s["maxed"], 1)
                dve.wait_ge(s["maxed"], m + 1)
                dve.tensor_scalar(nm, mx, -MLA_SCALE, None, ALU.mult).then_inc(s["negmax"], 1)
                dve.wait_ge(s["exps_done"], m + 1)
                dve.reciprocal(rc, sm).then_inc(s["rec_ready"], 1)
                dve.wait_ge(s["rec_ready"], m + 1)
                for j in range(2):
                    for t, (lo, hi) in enumerate(((0, 128), (128, 384))):
                        last = dve.tensor_scalar(pm[:, j, lo:hi], pm[:, j, lo:hi], rc[:, t, j:j + 1], None, ALU.mult)
                last.then_inc(s["p_ready"], 1)
                if proj:
                    rope_q(m + 1, 1 - p)
                dve.wait_ge(s["o_done"], m + 1)
                dve.tensor_copy(aT, pO[:, :, 0:T]).then_inc(s["o_ready"], 1)

            rope_q(0, 0)
            with dve.Fori(0, PAIRS - 3, 2) as m:
                mla_pair(m, 0)
                mla_pair(m + 1, 1)
            mla_pair(PAIRS - 2, 0)
            mla_pair(PAIRS - 1, 1, proj=False)
            dve.wait_ge(s["mla_done"], 1)
            link(dve.tensor_tensor(x1_sb[:, 0, :], x1_sb[:, 0, :], pD[:, :], ALU.add))
            link(dve.tensor_tensor(x1_sb[:, 1, :], x1_sb[:, 1, :], pP[:, :], ALU.add))

            norm(x1_sb, xn, 4).then_inc(s["xn_ready"], 1)
            dve.wait_ge(s["zc_ready"], 1)
            link(dve.tensor_copy(o2n_f, o2n_r[:, :]))
            link(dve.tensor_scalar(keep, o2n_f, -1.0, None, ALU.not_equal))
            link(dve.tensor_scalar(nkeep, keep, 1.0, -NEG, ALU.subtract, ALU.mult))
            link(dve.tensor_copy(o2n_cf, o2n_c[:, :]))
            link(dve.tensor_copy(iota_f, iota_i[:, :]))
            link(dve.tensor_scalar(emap, iota_f, o2n_cf, None, ALU.is_equal))
            dve.wait_ge(s["logits_done"], 1)
            for t in range(TT):
                link(dve.tensor_tensor(lm[:, t], pO[:, t, 0:NEXP], keep, ALU.mult))
                link(dve.tensor_tensor(lm[:, t], lm[:, t], nkeep, ALU.add))
                link(dve.max(top[:, t], lm[:, t]))
            dve.tensor_scalar(ntop, top[:, :, 0], -1.0, None, ALU.mult).then_inc(s["ntop_ready"], 1)
            for t in range(TT):
                link(dve.match_replace(rep[:, t], top[:, t], lm[:, t], 3.0 * NEG))
            link(dve.tensor_tensor(sel, rep, lm, ALU.not_equal))
            dve.nop().then_inc(s["sel_ready"], 1)
            dve.wait_ge(s["xh_ready"], 1)
            for c in range(HC):
                last = dve.scalar_tensor_tensor(xl[:, c], xT[:, c, :], SA, xh[:, c], ALU.mult, ALU.subtract)
            last.then_inc(s["xl_ready"], 1)
            dve.wait_ge(s["ex_ready"], 1)
            link(dve.tensor_tensor(ex, ex, sel, ALU.mult))
            link(dve.reduce_sum(zs, ex, AX.X))
            link(dve.reciprocal(zr, zs))
            link(dve.tensor_scalar(zr, zr, SH / (SA * SW), None, ALU.mult))
            dve.wait_ge(s["cnt_done"], 1)
            for t in range(TT):
                link(dve.tensor_scalar(rep[:, t], pO[:, t, 256:256 + NEXP], float(CAP), zr[:, t:t + 1], ALU.is_le, ALU.mult))
                link(dve.tensor_tensor(ex[:, t], ex[:, t], rep[:, t], ALU.mult))
            dve.nop().then_inc(s["w_ready"], 1)
            dve.wait_ge(s["wt_done"], 1)
            dve.tensor_copy(wT, pS[:, 2, 0:T]).then_inc(s["wt_ready"], 1)
            dve.wait_ge(s["wn_done"], 1)
            dve.tensor_copy(wnew[0:KEPT, :], pS[0:KEPT, 3, 0:T]).then_inc(s["wn_ready"], 1)

            def split_unit(n, slot, ring):
                dve.wait_ge(s["unit_hi"], n + 1)
                dve.scalar_tensor_tensor(uwl[:, ring], uw32[:, slot], SW, uwh[:, ring],
                                         ALU.mult, ALU.subtract).then_inc(s["unit_lo"], 1)

            def hidden(n, it, slot, bank, buf):
                dve.wait_ge(s["silu_ready"], n + 1)
                dve.tensor_tensor(m1[:, buf], pS[:, bank, T:2 * T], sg[:, buf], ALU.mult).then_inc(s["m1_ready"], 1)
                dve.wait_ge(wb_in[slot], 32 * (it + 1))
                dve.wait_ge(s["m1_ready"], n + 1)
                dve.tensor_tensor(m2[:, buf], m1[:, buf], wb[:, slot], ALU.mult).then_inc(s["m2_ready"], 1)
                dve.wait_ge(s["h_hi"], n + 1)
                dve.tensor_tensor(hl[:, buf], m2[:, buf], hh[:, buf], ALU.subtract).then_inc(s["h_lo"], 1)

            for n in range(2):
                split_unit(n, n, n)
            hidden(0, 0, 0, 0, 0)

            def moe_units(it, last_turn=False):
                for u in range(UNROLL):
                    n = UNROLL * it + u
                    if not (last_turn and u + 2 >= UNROLL):
                        dve.wait_ge(s["down_done"], n + 1)
                        split_unit(n + 2, (u + 2) % UNROLL, (u + 2) % 3)
                    if not (last_turn and u + 1 >= UNROLL):
                        hidden(n + 1, it + (u + 1) // UNROLL, (u + 1) % UNROLL, (u + 1) % 3, (u + 1) % 2)

            with dve.Fori(0, UNITS // UNROLL - 1) as it:
                moe_units(it)
            moe_units(UNITS // UNROLL - 1, last_turn=True)
            dve.wait_ge(s["moe_done"], 1)
            dve.scalar_tensor_tensor(work[:, 0, :], pD[:, :], 1.0 / (SH * SW), x1_sb[:, 0, :], ALU.mult, ALU.add)
            dve.scalar_tensor_tensor(work[:, 1, :], pP[:, :], 1.0 / (SH * SW), x1_sb[:, 1, :], ALU.mult, ALU.add)\
               .then_inc(s["out_ready"], 1)

        @block.tensor
        def _(pe):
            def mm(o, lhsT, rhs, start, stop, **kw):
                return pe.matmul(o, lhsT, rhs, start=start, stop=stop, **kw)

            def add_zero(banks, start, stop):
                for o in banks:
                    last = mm(o, zero16[:, 0:128], zero16[:, :], start, stop, skip_group_check=True)
                return last

            def transpose_rows(k):
                pe.wait_ge(s["xn_ready"], k)
                for t in range(TT):
                    for c in range(HC):
                        last = pe.transpose(pS[:, c // 2, 256 * (c % 2) + 128 * t:256 * (c % 2) + 128 * t + 128],
                                            xn[:, t, 128 * c:128 * c + 128], ident[:, :])
                last.then_inc(s["tr_done"], 1)

            pe.wait_ge(s["const_ready"], 1)
            transpose_rows(1)
            pe.wait_ge(s["wq_in"], 16)
            pe.wait_ge(s["xT_ready"], 1)
            for g in range(HC):
                for c in range(HC):
                    last = mm(pS[:, 2 + g // 2, 256 * (g % 2):256 * (g % 2) + 256], wqT[:, c, 128 * g:128 * g + 128],
                              xT[:, c, :], c == 0, c == HC - 1)
            last.then_inc(s["q_mm"], 1)

            def project(b, p, n, first=False):
                if n == 0:
                    pe.wait_ge(s["ctx_lo"], 4 * (b + 1))
                    if first:
                        pe.wait_ge(s["wk_lo"], 1)
                if not (first and n == 0):
                    pe.wait_ge(s["proj_evac"], 8 * b + n)
                k = 0
                for c in range(HC):
                    for wi, ci in ((0, chi), (1, chi), (0, clo)):
                        if n < HC:
                            last = mm(pP[:, :], wk16[:, wi, c, 128 * n:128 * n + 128], ci[:, p, c, :], k == 0, k == 11)
                        else:
                            r = n - HC
                            last = mm(pP[:, :], ci[:, p, c, 128 * r:128 * r + 128], wv16[:, wi, c, :], k == 0, k == 11)
                        k += 1
                last.then_inc(s["proj_done"], 1)

            for n in range(8):
                project(0, 0, n, first=True)
            add_zero((pO[:, 0, :], pO[:, 1, :], pD[:, :]), True, False)

            def scores(b, p, st):
                tile, g = st // HC, st % HC
                if st >= 2:
                    pe.wait_ge(s["exp_done"], STEPS * b + st - 1)
                for j in range(4):
                    last = mm(step_scores(st)[:, j, :], k_st[:, p, j, g, 128 * tile:128 * tile + 128],
                              q_st[:, j, g, :], True, True)
                last.then_inc(s["scores_done"], 1)

            def weigh(b, p, st):
                tile, g = st // HC, st % HC
                if g == 0:
                    pe.wait_ge(s["proj_evac"], 8 * b + HC + tile + 1)
                pe.wait_ge(s["clip_done"], STEPS * b + st + 1)
                for j in range(4):
                    mm(pO[32 * j:32 * j + 32, g // 2, 256 * (g % 2):256 * (g % 2) + 256],
                       v_sb[:, p, tile, 128 * g + 32 * j:128 * g + 32 * j + 32], probs[:, st % 2, j, :], False, False,
                       skip_group_check=True)
                for j in range(4):
                    last = mm(pD[32 * j:32 * j + 32, 0:T], onecol[:, g, :], probs[:, st % 2, j, :], False, False,
                              skip_group_check=True)
                last.then_inc(s["pv_done"], 1)

            def x_block(b, p, proj=True):
                pe.wait_ge(s["k_stacked"], 16 * STACK_DMAS * (b + 1))
                for st in range(STEPS):
                    scores(b, p, st)
                    if proj and st % 2 == 0:
                        project(b + 1, 1 - p, st // 2)
                    if st:
                        weigh(b, p, st - 1)
                weigh(b, p, STEPS - 1)

            pe.wait_ge(s["q_stacked"], 16 * 16)
            with pe.Fori(0, NBLK - 3, 2) as b:
                x_block(b, 0)
                x_block(b + 1, 1)
            x_block(NBLK - 2, 0)
            x_block(NBLK - 1, 1, proj=False)
            add_zero((pO[:, 0, :], pO[:, 1, :], pD[:, :]), False, True).then_inc(s["x_acc_done"], 1)

            pe.wait_ge(s["zc_ready"], 1)
            pe.wait_ge(s["den_ready"], 1)
            for g in range(HC):
                last = mm(pS[:, g // 2, 256 * (g % 2):256 * (g % 2) + 256], selrow[:, g, :], den, True, True)
            last.then_inc(s["denb_done"], 1)
            pe.wait_ge(s["ctxn_ready"], 1)
            pe.wait_ge(s["wo_in"], 16)
            for t in range(TT):
                for g in range(HC):
                    last = mm(pS[:, 2 + t, :], ctxn[:, g, 128 * t:128 * t + 128], woT[:, g, :], g == 0, g == HC - 1)
            last.then_inc(s["delta_done"], 1)

            transpose_rows(2)
            pe.wait_ge(s["xT_ready"], 2)
            pe.wait_ge(s["qa_in"], 16)
            pe.wait_ge(s["kva_in"], 16)
            for t in range(TT):
                for c in range(HC):
                    mm(pS[:, 2 + t, 0:QLR], xT[:, c, 128 * t:128 * t + 128], wqaT[:, c, :], c == 0, c == HC - 1)
                for c in range(HC):
                    mm(pO[:, 0, KVLR * t:KVLR * t + KVLR], xT[:, c, 128 * t:128 * t + 128], wkvaT[:, c, 0:KVLR],
                       c == 0, c == HC - 1)
            for r in range(2):
                for c in range(HC):
                    last = mm(pO[:, 1, T * r:T * r + T], wkvaT[:, c, KVLR + 128 * r:KVLR + 128 * r + 128], xT[:, c, :],
                              c == 0, c == HC - 1)
            last.then_inc(s["lat_mm"], 1)
            pe.wait_ge(s["latn_ready"], 1)
            for t in range(TT):
                for c in range(QC + 1):
                    src = cqn[:, t, 128 * c:128 * c + 128] if c < QC else kvn[:, t, :]
                    last = pe.transpose(pS[:, c // 2, 256 * (c % 2) + 128 * t:256 * (c % 2) + 128 * t + 128], src, ident[:, :])
            last.then_inc(s["lat_tr"], 1)
            pe.wait_ge(s["lat_ready"], 1)
            pe.wait_ge(s["kpe_ready"], 1)
            add_zero((pD[:, :], pP[:, :]), True, False)

            def proj_q(m, p, first=False):
                if not first:
                    pe.wait_ge(s["qkv_ready"], 3 * m)
                    pe.wait_ge(s["rope_ready"], m)
                pe.wait_ge(min_in[p], 16 * (m // 2 + 1) if isinstance(m, int) else 8 * (m - p) + 16)
                w = mw_in[:, p, 0:QC * 512].rearrange("p (c n) -> p c n", c=QC)
                for r in range(2):
                    for j in range(2):
                        for c in range(QC):
                            last = mm(pS[:, r, T * j:T * j + T], w[:, c, 256 * r + 128 * j:256 * r + 128 * j + 128],
                                      lat[:, c, :], c == 0, c == QC - 1)
                    last.then_inc(s["mproj_done"], 1)

            def proj_kv(m, p):
                w = mw_in[:, p, QC * 512:QC * 512 + 512]
                for j in range(2):
                    last = mm(pS[:, 2, T * j:T * j + T], w[:, 128 * j:128 * j + 128], lat[:, QC, :], True, True)
                last.then_inc(s["mproj_done"], 1)
                for t in range(TT):
                    last = mm(pS[:, 3, T * t:T * t + T], lat[:, QC, 128 * t:128 * t + 128], w[:, 256:512], True, True)
                last.then_inc(s["mproj_done"], 1)

            def mla_scores(m, p):
                pe.wait_ge(s["qkv_ready"], 3 * m + 2)
                pe.wait_ge(s["rope_ready"], m + 1)
                for j in range(2):
                    for t, (lo, hi) in enumerate(((0, 128), (128, 384))):
                        mm(pO[:, j, lo:hi], qn[:, p, j, 128 * t:128 * t + 128], kn[:, p, j, 0:hi - lo], True, False)
                        last = mm(pO[:, j, lo:hi], qpe[64 * j:64 * j + 64, p, 128 * t:128 * t + 128],
                                  kpe[64 * j:64 * j + 64, 0:hi - lo], False, True)
                last.then_inc(s["s_done"], 1)

            def mla_pair(m, p, proj=True):
                mla_scores(m, p)
                if proj:
                    proj_q(m + 1, 1 - p)
                pe.wait_ge(s["p_ready"], m + 1)
                for j in range(2):
                    for i in range(3):
                        last = pe.transpose(pO[:, j, 128 * i:128 * i + 128], pm[:, j, 128 * i:128 * i + 128], ident[:, :])
                last.then_inc(s["pt_done"], 1)
                if proj:
                    proj_kv(m + 1, 1 - p)
                pe.wait_ge(s["pt_ready"], m + 1)
                pe.wait_ge(s["qkv_ready"], 3 * m + 3)
                for j in range(2):
                    mm(pO[:, j, 0:T], vv[:, p, 0, 128 * j:128 * j + 128], pt[:, j, 0:T], True, False)
                    last = mm(pO[:, j, 128:T], vv[:, p, 1, 128 * j:128 * j + 128], pt[:, j, T:384], False, True)
                last.then_inc(s["o_done"], 1)
                pe.wait_ge(s["o_ready"], m + 1)
                pe.wait_ge(mout_in[p], 16 * (m // 2 + 1) if isinstance(m, int) else 8 * (m - p) + 16)
                for t, o in enumerate((pD, pP)):
                    for j in range(2):
                        last = mm(o[:, :], aT[:, j, 128 * t:128 * t + 128], mw_out[:, p, 512 * j:512 * j + 512],
                                  False, False, skip_group_check=True)
                last.then_inc(s["wo_done"], 1)

            proj_q(0, 0, first=True)
            proj_kv(0, 0)
            with pe.Fori(0, PAIRS - 3, 2) as m:
                mla_pair(m, 0)
                mla_pair(m + 1, 1)
            mla_pair(PAIRS - 2, 0)
            mla_pair(PAIRS - 1, 1, proj=False)
            add_zero((pD[:, :], pP[:, :]), False, True).then_inc(s["mla_done"], 1)

            transpose_rows(3)
            pe.wait_ge(s["xT_ready"], 3)
            pe.wait_ge(s["gate_in"], 16)
            for t in range(TT):
                for c in range(HC):
                    last = mm(pO[:, t, 0:NEXP], xT[:, c, 128 * t:128 * t + 128], gateT[:, c, :], c == 0, c == HC - 1)
            last.then_inc(s["logits_done"], 1)
            pe.wait_ge(s["sel_ready"], 1)
            mm(pO[:, 0, 256:256 + NEXP], tri[:, :], sel[:, 0], True, True)
            mm(pO[:, 1, 256:256 + NEXP], ones[:, :], sel[:, 0], True, False)
            mm(pO[:, 1, 256:256 + NEXP], tri[:, :], sel[:, 1], False, True).then_inc(s["cnt_done"], 1)
            pe.wait_ge(s["w_ready"], 1)
            for t in range(TT):
                last = pe.transpose(pS[:, 2, 128 * t:128 * t + 128], ex[:, t], ident[:, :])
            last.then_inc(s["wt_done"], 1)
            pe.wait_ge(s["wt_ready"], 1)
            mm(pS[0:KEPT, 3, 0:T], emap, wT, True, True).then_inc(s["wn_done"], 1)

            add_zero((pD[:, :], pP[:, :]), True, False).then_inc(s["down_done"], 1)

            def gate_up(n, bank, ring):
                pe.wait_ge(s["unit_lo"], n + 1)
                for half in range(2):
                    k = 0
                    for c in range(HC):
                        for w, x in ((uwh, xh), (uwl, xh), (uwh, xl)):
                            last = mm(pS[:, bank, T * half:T * half + T],
                                      w[:, ring, 256 * c + 128 * half:256 * c + 128 * half + 128], x[:, c, :], k == 0, k == 11)
                            k += 1
                last.then_inc(s["gu_done"], 1)

            def down(n, ring, buf):
                pe.wait_ge(s["h_lo"], n + 1)
                for t, o in enumerate((pD, pP)):
                    for h, w in ((hh, uwh), (hh, uwl), (hl, uwh)):
                        last = mm(o[:, :], h[:, buf, 128 * t:128 * t + 128], w[:, ring, HC * 256:UW], False, False,
                                  skip_group_check=True)
                last.then_inc(s["down_done"], 1)

            pe.wait_ge(s["xl_ready"], 1)
            gate_up(0, 0, 0)

            def moe_units(it, last_turn=False):
                for u in range(UNROLL):
                    n = UNROLL * it + u
                    if not (last_turn and u + 1 >= UNROLL):
                        gate_up(n + 1, (u + 1) % 3, (u + 1) % 3)
                    down(n, u % 3, u % 2)

            with pe.Fori(0, UNITS // UNROLL - 1) as it:
                moe_units(it)
            moe_units(UNITS // UNROLL - 1, last_turn=True)
            add_zero((pD[:, :], pP[:, :]), False, True).then_inc(s["moe_done"], 1)


def q_f32(probs, g):
    return probs[:, g // 2, 2 * (g % 2), :]


def kernel(**inputs):
    import numpy as _np
    import concourse.bacc as _bacc
    from concourse import mybir as _mybir
    from concourse.bass_utils import run_bass_kernel_spmd as _run

    v = {k: _np.asarray(t) for k, t in inputs.items()}

    def chunked(wT):
        return wT.reshape(-1, 128, wT.shape[1]).transpose(1, 0, 2)

    def by_channel(vec):
        return vec.reshape(-1, 128).T

    P = "L0_xattn_"
    A = "L0_attn_"
    F = "L0_ffn_"
    arrays = {
        "x": v["x"][0].reshape(TT, 128, HID).transpose(1, 0, 2),
        "ctxT": v["ctx_2048"][0].reshape(NBLK, CB, HC, 128).transpose(0, 3, 2, 1),
        "mask": v["mask_BxS2_ik0"][0].reshape(S2 // 128, 128).T,
        "wqT": chunked(v[P + "Wq"].T), "wkT": chunked(v[P + "Wk"].T), "wvT": chunked(v[P + "Wv"].T),
        "woT": chunked(v[P + "Wo"].T),
        "xb": _np.stack([by_channel(v[P + b]) for b in ("bq", "bk", "bv")], axis=1),
        "bo": v[P + "bo"][None], "gamma": v[P + "ln_gamma"][None], "beta": v[P + "ln_beta"][None],
        "rs": v[P + "residual_scale"].reshape(1, 1),
        "wqaT": chunked(v[A + "w_qa"].T),
        "lnw": _np.concatenate([by_channel(v[A + "q_a_ln_w"]), by_channel(v[A + "kv_a_ln_w"])], axis=1),
        "gateT": chunked(v[F + "gate_weight"].T),
        "o2n_c": v[F + "old_to_new"].reshape(NEXP, 1), "o2n_r": v[F + "old_to_new"].reshape(1, NEXP),
    }
    half = DR // 2
    swap = _np.r_[half:DR, 0:half]
    pe_rows = v[A + "w_kva"][KVLR:]
    arrays["wkvaT"] = chunked(_np.concatenate(
        [v[A + "w_kva"][:KVLR], pe_rows, pe_rows, pe_rows[swap], pe_rows[swap]]).T)
    wqb = v[A + "w_qb"].reshape(PAIRS, 2, DN + DR, QLR)
    wkvb = v[A + "w_kvb"].reshape(PAIRS, 2, DN + DV, KVLR)
    qrows = _np.concatenate([wqb[:, 0, :DN], wqb[:, 1, :DN], wqb[:, 0, DN:], wqb[:, 1, DN:],
                             wqb[:, 0, DN:][:, swap], wqb[:, 1, DN:][:, swap]], axis=1)
    kvrows = _np.concatenate([wkvb[:, 0, :DN], wkvb[:, 1, :DN], wkvb[:, 0, DN:], wkvb[:, 1, DN:]], axis=1)
    arrays["mla_in"] = _np.concatenate(
        [qrows.transpose(0, 2, 1).reshape(PAIRS, QC, 128, 512).transpose(0, 2, 1, 3).reshape(PAIRS, 128, QC * 512),
         kvrows.transpose(0, 2, 1)], axis=2)
    arrays["mla_out"] = v[A + "w_o"].T.reshape(PAIRS, 2, 128, HID).transpose(0, 2, 1, 3).reshape(PAIRS, 128, 2 * HID)
    inv = (1.0 / _np.float32(10000.0) ** (_np.arange(0, DR, 2, dtype=_np.float32) / _np.float32(DR))).astype(_np.float32)
    angle = _np.outer(_np.arange(T, dtype=_np.float32), inv).astype(_np.float32).T
    cos, sin = _np.cos(angle), _np.sin(angle)
    arrays["cosT"] = _np.concatenate([cos] * 4)
    arrays["sinT"] = _np.concatenate([-sin, sin] * 2)
    gu = v[F + "gate_up_proj"].reshape(KEPT // 2, 2, 2, INTER, HID)
    dn = v[F + "down_proj"].reshape(KEPT // 2, 2, HID, INTER)
    rows = [gu[:, 0, :, :128], gu[:, 1, :, :128], _np.concatenate([gu[:, 0, :, 128:], gu[:, 1, :, 128:]], axis=2)]
    cols = [dn[:, 0, :, :128], dn[:, 1, :, :128], _np.concatenate([dn[:, 0, :, 128:], dn[:, 1, :, 128:]], axis=2)]
    gu_u = _np.stack(rows, axis=1).reshape(UNITS, 256, HC, 128).transpose(0, 3, 2, 1).reshape(UNITS, 128, HC * 256)
    dn_u = _np.stack(cols, axis=1).reshape(UNITS, HID, 128).transpose(0, 2, 1)
    arrays["units"] = _np.concatenate([gu_u, dn_u], axis=2)

    nc = _bacc.Bacc("TRN2", target_bir_lowering=False, num_devices=1)
    arrays = {k: _np.ascontiguousarray(t) for k, t in arrays.items()}
    aps = {k: nc.dram_tensor("in_" + k, t.shape, _mybir.dt.from_np(t.dtype), kind="ExternalInput").ap()
           for k, t in arrays.items()}
    out = nc.dram_tensor("out_0", (128, TT, HID), _mybir.dt.float32, kind="ExternalOutput").ap()
    build(nc, aps, out)
    r = _run(nc, [{"in_" + k: t for k, t in arrays.items()}], core_ids=[0])
    return r.results[0]["out_0"].transpose(1, 0, 2).reshape(1, T, HID)
```

```python
import concourse.bass as bass
from concourse import mybir
from contextlib import ExitStack
import numpy as np


T, HID = 256, 512
TT, HC = T // 128, HID // 128
S2 = 4096
XH, XD = 16, 32
CB = 512
NBLK, CT = S2 // CB, CB // 128
STEPS = CT * HC
QLR, KVLR, DN, DR, DV = 384, 128, 128, 64, 128
MH = 16
PAIRS = MH // 2
QC = QLR // 128
NEXP, KEPT, TOPK, INTER, CAP = 128, 48, 8, 192, 192
UNITS = KEPT * INTER // 128
UNROLL = 12
RING = 4
AHEAD = RING - 1
UW = HC * 256 + HID
SA, SW, SH = 64.0, 256.0, 16.0
NEG = -1.0e30
MLA_SCALE = float(DN + DR) ** -0.5
X_SCALE = float(XD) ** -0.5


def build(nc, a, out):
    f32, f16, i32 = mybir.dt.float32, mybir.dt.float16, mybir.dt.int32
    ALU, ACT, AX = mybir.AluOpType, mybir.ActivationFunctionType, mybir.AxisListType

    ctx = ExitStack()
    with ctx:
        def sb(name, shape, dt=f32):
            return ctx.enter_context(nc.sbuf_tensor(name, shape, dt))

        def sem(name):
            return ctx.enter_context(nc.semaphore(name))

        pS = ctx.enter_context(nc.psum_tensor("pS", [128, 4, 512], f32))
        pO = ctx.enter_context(nc.psum_tensor("pO", [128, 2, 512], f32))
        pD = ctx.enter_context(nc.psum_tensor("pD", [128, 512], f32))
        pP = ctx.enter_context(nc.psum_tensor("pP", [128, 512], f32))

        def step_scores(st):
            return pS[:, 2 * (st % 2):2 * (st % 2) + 2, :].rearrange("p b (h q) -> p (b h) q", h=2)

        x_sb = sb("x_sb", [128, TT, HID])
        x1_sb = sb("x1_sb", [128, TT, HID])
        xn = sb("xn", [128, TT, HID])
        xT = sb("xT", [128, HC, T])
        work = sb("work", [128, 2, HID])
        bo_b = sb("bo_b", [128, HID])
        gam_b = sb("gam_b", [128, HID])
        bet_b = sb("bet_b", [128, HID])
        wqaT = sb("wqaT", [128, HC, QLR])
        wkvaT = sb("wkvaT", [128, HC, KVLR + 256])
        xb = sb("xb", [128, 3, HC])
        lnw = sb("lnw", [128, QC + 1])
        rs = sb("rs", [128, 1])
        mask_i = sb("mask_i", [128, S2 // 128], i32)
        mtab = sb("mtab", [128, NBLK, 2, CT])
        mblk = sb("mblk", [128, 2, 2, CT])
        o2n_c = sb("o2n_c", [128, 1], i32)
        o2n_r = sb("o2n_r", [128, NEXP], i32)
        ident = sb("ident", [128, 128])
        ones = sb("ones", [128, 128])
        tri = sb("tri", [128, 128])
        cmask = sb("cmask", [128, 128])
        zero16 = sb("zero16", [128, 512], f16)
        onecol = sb("onecol", [128, HC, 32])
        selrow = sb("selrow", [128, HC, 128])
        iota_i = sb("iota_i", [128, KEPT], i32)
        nhalf = sb("nhalf", [128, 2])
        bn = sb("bn", [128, TT, 6])
        mv = sb("mv", [128, TT, 2])
        var = sb("var", [128, TT])
        rstd = sb("rstd", [128, TT])
        mw_in = sb("mw_in", [128, 2, QC * 512 + 512])
        mw_out = sb("mw_out", [128, 2, 1024])

        ARENA = 34816
        arena = sb("arena", [128, ARENA])
        at = [0]

        def take(n, dt=f32):
            words = n if dt == f32 else n // 2
            v = arena[:, at[0]:at[0] + words]
            at[0] += words
            assert at[0] <= ARENA
            return v if dt == f32 else v.bitcast(dt)

        cbuf = take(2 * HC * CB).rearrange("p (b c t) -> p b c t", b=2, c=HC)
        chi = take(2 * HC * CB, f16).rearrange("p (b c t) -> p b c t", b=2, c=HC)
        clo = take(2 * HC * CB, f16).rearrange("p (b c t) -> p b c t", b=2, c=HC)
        wk16 = take(2 * HC * HID, f16).rearrange("p (s c n) -> p s c n", s=2, c=HC)
        wv16 = take(2 * HC * HID, f16).rearrange("p (s c n) -> p s c n", s=2, c=HC)
        kh = take(HC * CB, f16).rearrange("p (g t) -> p g t", g=HC)
        kl = take(HC * CB, f16).rearrange("p (g t) -> p g t", g=HC)
        kf = take(2 * CB).rearrange("p (b t) -> p b t", b=2)
        v_sb = take(2 * CT * HID).rearrange("p (b t n) -> p b t n", b=2, t=CT)
        woT = cbuf[:, 0]
        wqT = v_sb[:, 1]
        q_st = take(XH * T, f16).rearrange("p (j g q) -> p j g q", j=4, g=HC)
        probs = take(CT * 4 * T).rearrange("p (b j q) -> p b j q", b=CT, j=4)
        psum4 = take(4 * T).rearrange("p (j q) -> p j q", j=4)
        k_at = at[0]
        k_st = take(2 * XH * CB, f16).rearrange("p (b j g t) -> p b j g t", b=2, j=4, g=HC)
        wk32 = arena[:, k_at + 4096:k_at + 6144].rearrange("p (c n) -> p c n", c=HC)
        wv32 = arena[:, k_at + 6144:k_at + 8192].rearrange("p (c n) -> p c n", c=HC)
        qh, ql = (work[:, i, :].bitcast(f16).rearrange("p (g q) -> p g q", g=HC) for i in range(2))
        x_end = at[0]
        at[0] = 0
        uw32 = take(RING * UW).rearrange("p (b n) -> p b n", b=RING)
        uwh = take(RING * UW, f16).rearrange("p (b n) -> p b n", b=RING)
        uwl = take(RING * UW, f16).rearrange("p (b n) -> p b n", b=RING)
        wb = take(RING * T).rearrange("p (b t) -> p b t", b=RING)
        xh = take(HC * T, f16).rearrange("p (c t) -> p c t", c=HC)
        xl = take(HC * T, f16).rearrange("p (c t) -> p c t", c=HC)
        sg = take(2 * T).rearrange("p (b t) -> p b t", b=2)
        m1 = take(2 * T).rearrange("p (b t) -> p b t", b=2)
        m2 = take(2 * T).rearrange("p (b t) -> p b t", b=2)
        hh = take(2 * T, f16).rearrange("p (b t) -> p b t", b=2)
        hl = take(2 * T, f16).rearrange("p (b t) -> p b t", b=2)
        ctxn = take(HC * T).rearrange("p (g q) -> p g q", g=HC)
        rden = take(HC * T).rearrange("p (g q) -> p g q", g=HC)
        den = take(T)
        lat_at = at[0]
        cqn = take(TT * QLR).rearrange("p (t n) -> p t n", t=TT)
        kvn = take(TT * KVLR).rearrange("p (t n) -> p t n", t=TT)
        ssq = take(2 * TT)
        lrs = take(2 * TT)
        lat = take((QC + 1) * T).rearrange("p (c t) -> p c t", c=QC + 1)
        kpe = take(T)
        rp1 = take(T)
        rp2 = take(T)
        qn = take(4 * T).rearrange("p (b j t) -> p b j t", b=2, j=2)
        kn = take(4 * T).rearrange("p (b j t) -> p b j t", b=2, j=2)
        vv = take(4 * T).rearrange("p (b t n) -> p b t n", b=2, t=TT)
        qpe = take(2 * T).rearrange("p (b t) -> p b t", b=2)
        pm = take(2 * 384).rearrange("p (j k) -> p j k", j=2)
        pt = take(2 * 384).rearrange("p (j k) -> p j k", j=2)
        ah = take(2 * T, f16).rearrange("p (j t) -> p j t", j=2)
        al = take(2 * T, f16).rearrange("p (j t) -> p j t", j=2)
        woh = take(4 * HID, f16).rearrange("p (b n) -> p b n", b=2)
        wol = take(4 * HID, f16).rearrange("p (b n) -> p b n", b=2)
        mwh, mwl = take((QC + 1) * 512, f16), take((QC + 1) * 512, f16)
        lath, latl = (arena[:, lat_at + i * (QC + 1) * T // 2:lat_at + (i + 1) * (QC + 1) * T // 2].bitcast(f16)
                      .rearrange("p (c t) -> p c t", c=QC + 1) for i in range(2))
        q_part, kv_part = slice(0, QC * 512), slice(QC * 512, (QC + 1) * 512)
        mx = take(4).rearrange("p (t j) -> p t j", t=2)
        nm = take(4).rearrange("p (t j) -> p t j", t=2)
        sm = take(4).rearrange("p (t j) -> p t j", t=2)
        rc = take(4).rearrange("p (t j) -> p t j", t=2)
        cosT, sinT = take(T), take(T)
        gateT = take(HC * NEXP).rearrange("p (c n) -> p c n", c=HC)
        keep = take(NEXP)
        nkeep = take(NEXP)
        o2n_f = take(NEXP)
        o2n_cf = take(1)
        iota_f = take(KEPT)
        emap = take(KEPT)
        lm = take(TT * NEXP).rearrange("p (t n) -> p t n", t=TT)
        rep = take(TT * NEXP).rearrange("p (t n) -> p t n", t=TT)
        sel = take(TT * NEXP).rearrange("p (t n) -> p t n", t=TT)
        ex = take(TT * NEXP).rearrange("p (t n) -> p t n", t=TT)
        top = take(TT * TOPK).rearrange("p (t n) -> p t n", t=TT)
        ntop = take(TT)
        zs = take(TT)
        zr = take(TT)
        wT = take(T)
        wnew = take(T)
        assert x_end <= ARENA

        wdram = nc.dram_tensor("w_scratch", [KEPT, T], f32, kind="Internal").ap()

        names = """x_in small_in row_in wq_in wk_in wv_in wo_in gate_in qa_in kva_in rope_in
            var_ready rstd_ready xn_ready tr_done xT_ready
            const_ready zc_ready prep_ready wk_hi wk_lo q_mm q_f q_hi q_lo q_stacked
            ctx_hi ctx_lo proj_done proj_evac k_hi k_lo k_stacked
            scores_done exp_done clip_done sum_done dsum_done
            x_acc_done den_ready denb_done rden_ready ctxn_ready delta_done
            lat_mm ssq_ready lvar_ready lrstd_ready latn_ready lat_tr lat_ready lat_hi lat_lo mq_hi mq_lo mkv_hi mkv_lo kpe_ready rope_step
            mproj_done qkv_ready rope_ready s_done masked maxed negmax exps_done rec_ready p_ready
            pt_done pt_ready o_done a_hi a_lo wo_hi wo_lo mla_done
            xh_ready xl_ready logits_done ntop_ready ex_ready sel_ready
            cnt_done w_ready wt_done wt_ready wn_done wn_ready w_stored
            unit_hi unit_lo gu_done silu_ready m1_ready m2_ready h_hi h_lo down_done moe_done
            out_ready out_stored dch pch ach""".split()
        s = {n: sem(n) for n in names}
        ctx_in = [sem(f"ctx_in{i}") for i in range(2)]
        mblk_in = [sem(f"mblk_in{i}") for i in range(2)]
        min_in = [sem(f"mla_in{i}") for i in range(2)]
        mout_in = [sem(f"mla_out_in{i}") for i in range(2)]
        unit_in = [sem(f"unit_in{i}") for i in range(RING)]
        wb_in = [sem(f"wb_in{i}") for i in range(RING)]

        STACK_DMAS = 16
        block = ctx.enter_context(nc.Block())

        @block.sync
        def _(sp):
            def load_ctx(b, p):
                sp.dma_start(cbuf[:, p], a["ctxT"][b]).then_inc(ctx_in[p], 16)

            def load_mask(b, p):
                sp.dma_start(mblk[:, p], mtab[:, b]).then_inc(mblk_in[p], 16)

            def stack_k(b, p):
                sp.wait_ge(s["k_lo"], 4 * (b + 1))
                for j in range(4):
                    for part, src in ((0, kh), (1, kl), (2, kh), (3, kl)):
                        sp.dma_start(k_st[32 * part:32 * part + 32, p, j], src[32 * j:32 * j + 32, :, :])\
                          .then_inc(s["k_stacked"], 16)

            def load_mla_in(m, p):
                sp.dma_start(mw_in[:, p], a["mla_in"][m]).then_inc(min_in[p], 16)

            def load_mla_out(m, p):
                sp.dma_start(mw_out[:, p], a["mla_out"][m]).then_inc(mout_in[p], 16)

            def load_unit(n, slot):
                sp.dma_start(uw32[:, slot], a["units"][n]).then_inc(unit_in[slot], 16)

            def load_wb(it, u):
                pair, kind = UNROLL // 3 * it + u // 3, u % 3
                for half in range(2):
                    e = 2 * pair + (half if kind == 2 else kind)
                    sp.dma_start(wb[64 * half:64 * half + 64, u % RING],
                                 wdram[e, :].unsqueeze(0).broadcast_to([64, T])).then_inc(wb_in[u % RING], 16)

            sp.dma_start(x_sb[:, :, :], a["x"]).then_inc(s["x_in"], 16)
            sp.dma_start(wk32, a["wkT"]).then_inc(s["wk_in"], 16)
            sp.dma_start(wqT, a["wqT"]).then_inc(s["wq_in"], 16)
            load_ctx(0, 0)
            sp.dma_start(wv32, a["wvT"]).then_inc(s["wv_in"], 16)
            load_ctx(1, 1)
            sp.dma_start(wqaT[:, :, :], a["wqaT"]).then_inc(s["qa_in"], 16)
            sp.dma_start(wkvaT[:, :, :], a["wkvaT"]).then_inc(s["kva_in"], 16)
            for m in range(2):
                load_mla_in(m, m)
                load_mla_out(m, m)
            stack_k(0, 0)
            sp.wait_ge(s["prep_ready"], 1)
            load_mask(0, 0)

            def x_block(b, p, stack=True, load=True):
                if load:
                    sp.wait_ge(s["ctx_lo"], 4 * (b + 1))
                    sp.nop()
                    load_ctx(b + 2, p)
                if stack:
                    sp.wait_ge(s["exp_done"], STEPS * b + 1)
                    sp.nop()
                    load_mask(b + 1, 1 - p)
                    stack_k(b + 1, 1 - p)

            with sp.Fori(0, NBLK - 3, 2) as b:
                x_block(b, 0)
                x_block(b + 1, 1)
            x_block(NBLK - 2, 0, load=False)

            sp.wait_ge(s["ctx_lo"], 4 * (NBLK - 1))
            sp.dma_start(woT, a["woT"]).then_inc(s["wo_in"], 16)

            sp.wait_ge(s["x_acc_done"], 1)
            sp.dma_start(cosT, a["cosT"]).then_inc(s["rope_in"], 16)
            sp.dma_start(sinT, a["sinT"]).then_inc(s["rope_in"], 16)
            sp.dma_start(gateT, a["gateT"]).then_inc(s["gate_in"], 16)
            sp.wait_ge(s["delta_done"], TT)
            for n in range(RING):
                load_unit(n, n)

            with sp.Fori(0, PAIRS - 3, 2) as m:
                for p in range(2):
                    sp.wait_ge(s["mkv_lo"], m + p + 1)
                    sp.nop()
                    load_mla_in(m + p + 2, p)
                    sp.wait_ge(s["wo_lo"], m + p + 1)
                    sp.nop()
                    load_mla_out(m + p + 2, p)

            sp.wait_ge(s["wn_ready"], 1)
            sp.dma_start(wdram, wnew[0:KEPT, :]).then_inc(s["w_stored"], 16)
            sp.wait_ge(s["w_stored"], 16)
            for u in range(RING):
                load_wb(0, u)

            def moe_loads(it, count):
                for u in range(count):
                    n = UNROLL * it + u
                    sp.wait_ge(s["unit_lo"], n + 1)
                    sp.nop()
                    load_unit(n + RING, u % RING)
                    sp.wait_ge(s["m2_ready"], n + 1)
                    sp.nop()
                    load_wb(it, u + RING)

            with sp.Fori(0, UNITS // UNROLL - 1) as it:
                moe_loads(it, UNROLL)
            moe_loads(UNITS // UNROLL - 1, UNROLL - RING)

            sp.wait_ge(s["out_ready"], 1)
            sp.dma_start(out, work[:, :, :]).then_inc(s["out_stored"], 16)
            sp.wait_ge(s["out_stored"], 16)

        @block.gpsimd
        def _(pool):
            chain = [0]

            def link(ins):
                chain[0] += 1
                ins.then_inc(s["pch"], 1)
                pool.wait_ge(s["pch"], chain[0])

            pool.memset(nhalf[:, :], -0.5).then_inc(s["pch"], 1)
            pool.memset(ident[:, :], 0.0).then_inc(s["pch"], 1)
            pool.memset(zero16[:, :], 0.0).then_inc(s["pch"], 1)
            pool.memset(onecol[:, :, :], 0.0).then_inc(s["pch"], 1)
            pool.memset(selrow[:, :, :], 0.0).then_inc(s["pch"], 1)
            pool.memset(ones[:, :], 1.0).then_inc(s["pch"], 1)
            pool.memset(tri[:, :], 1.0).then_inc(s["pch"], 1)
            chain[0] = 7
            link(pool.memset(cmask[:, :], 0.0))
            link(pool.affine_select(out=ident[:, :], in_=ident[:, :], compare_op=ALU.not_equal, fill=1.0, base=0,
                                    pattern=[[-1, 128]], channel_multiplier=1))
            for g in range(HC):
                link(pool.memset(onecol[:, g, g:g + 1], 1.0))
            pool.nop().then_inc(s["const_ready"], 1)

            pool.wait_ge(s["var_ready"], 1)
            pool.tensor_tensor(rstd[:, :], var[:, :], nhalf[:, :], ALU.pow).then_inc(s["rstd_ready"], 1)

            pool.wait_ge(s["q_lo"], 1)
            for j in range(4):
                for part, src in ((0, qh), (1, qh), (2, ql), (3, ql)):
                    pool.dma_start(q_st[32 * part:32 * part + 32, j], src[32 * j:32 * j + 32]).then_inc(s["q_stacked"], 16)

            link(pool.affine_select(out=selrow[:, :, :].rearrange("p g (j m) -> p g j m", j=4),
                                    in_=selrow[:, :, :].rearrange("p g (j m) -> p g j m", j=4),
                                    compare_op=ALU.not_equal, fill=1.0, base=0,
                                    pattern=[[-1, HC], [-32, 4], [0, 32]], channel_multiplier=1))
            link(pool.affine_select(out=tri[:, :], in_=tri[:, :], compare_op=ALU.is_ge, fill=0.0, base=0,
                                    pattern=[[1, 128]], channel_multiplier=-1))
            link(pool.affine_select(out=cmask[:, :], in_=cmask[:, :], compare_op=ALU.is_ge, fill=NEG, base=0,
                                    pattern=[[-1, 128]], channel_multiplier=1))
            link(pool.iota(iota_i[:, :], pattern=[[1, KEPT]], base=0, channel_multiplier=0))
            pool.nop().then_inc(s["zc_ready"], 1)
            pool.wait_ge(s["var_ready"], 2)
            pool.tensor_tensor(rstd[:, :], var[:, :], nhalf[:, :], ALU.pow).then_inc(s["rstd_ready"], 1)
            pool.wait_ge(s["var_ready"], 3)
            pool.tensor_tensor(rstd[:, :], var[:, :], nhalf[:, :], ALU.pow).then_inc(s["rstd_ready"], 1)
            pool.wait_ge(s["lvar_ready"], 1)
            for i in range(2):
                last = pool.tensor_tensor(lrs[:, TT * i:TT * i + TT], ssq[:, TT * i:TT * i + TT], nhalf[:, :], ALU.pow)
            last.then_inc(s["lrstd_ready"], 1)
            pool.wait_ge(s["var_ready"], 4)
            pool.tensor_tensor(rstd[:, :], var[:, :], nhalf[:, :], ALU.pow).then_inc(s["rstd_ready"], 1)

        @block.scalar
        def _(act):
            def transposed(k):
                act.wait_ge(s["tr_done"], k)
                for i in range(2):
                    last = act.activation(xT[:, 2 * i:2 * i + 2, :], pS[:, i, :].rearrange("p (c t) -> p c t", c=2), ACT.Copy)
                last.then_inc(s["xT_ready"], 1)

            def split_ctx(p, c):
                act.activation(chi[:, p, c], cbuf[:, p, c], ACT.Copy, scale=SA).then_inc(s["ctx_hi"], 1)

            for dst, src in ((xb[:, :, :], a["xb"]), (lnw[:, :], a["lnw"]), (mask_i[:, :], a["mask"]),
                             (rs[:, :], a["rs"].broadcast_to([128, 1])), (o2n_c[:, :], a["o2n_c"]),
                             (o2n_r[:, :], a["o2n_r"].broadcast_to([128, NEXP]))):
                act.dma_start(dst, src).then_inc(s["small_in"], 16)
            for dst, src in ((bo_b, "bo"), (gam_b, "gamma"), (bet_b, "beta")):
                act.dma_start(dst[:, :], a[src].broadcast_to([128, HID])).then_inc(s["row_in"], 16)
            act.wait_ge(s["wk_in"], 16)
            act.activation(wk16[:, 0], wk32, ACT.Copy, scale=SW).then_inc(s["wk_hi"], 1)
            transposed(1)
            act.wait_ge(ctx_in[0], 16)
            for c in range(HC):
                split_ctx(0, c)
            act.wait_ge(s["wv_in"], 16)
            act.activation(wv16[:, 0], wv32, ACT.Copy, scale=SW).then_inc(s["wk_hi"], 1)
            act.wait_ge(s["q_mm"], 1)
            act.wait_ge(s["prep_ready"], 1)
            for g in range(HC):
                last = act.activation(q_f32(probs, g), pS[:, 2 + g // 2, 256 * (g % 2):256 * (g % 2) + 256],
                                      ACT.Identity, bias=xb[:, 0, g:g + 1], scale=SA)
            last.then_inc(s["q_f"], 1)

            def evac(b, p, n, first=False):
                act.wait_ge(s["proj_done"], 8 * b + n + 1)
                if n < HC:
                    if not (first and n < 2):
                        act.wait_ge(s["k_lo"], 4 * b + n - 1)
                    act.activation(kf[:, n % 2], pP[:, :], ACT.Identity, bias=xb[:, 1, n:n + 1],
                                   scale=1.0 / SW).then_inc(s["proj_evac"], 1)
                else:
                    act.activation(v_sb[:, p, n - HC], pP[:, :], ACT.Copy,
                                   scale=1.0 / (SA * SW)).then_inc(s["proj_evac"], 1)

            for n in range(8):
                evac(0, 0, n, first=True)
                if n == 3:
                    act.wait_ge(ctx_in[1], 16)
                if n >= 3 and n < 7:
                    split_ctx(1, n - 3)

            def x_block(b, p, proj=True, split=True):
                for st in range(STEPS):
                    if proj and st % 2:
                        evac(b + 1, 1 - p, st // 2)
                    act.wait_ge(s["scores_done"], STEPS * b + st + 1)
                    if st == 0:
                        act.wait_ge(mblk_in[p], 16 * (b // 2 + 1) if isinstance(b, int) else 8 * (b - p) + 16)
                    g, tile = st // CT, st % CT
                    if g:
                        act.wait_ge(s["sum_done"], 12 * b + 3 * (g - 1) + max(1, tile))
                    act.activation(probs[:, tile], step_scores(st), ACT.Exp,
                                   bias=mblk[:, p, 1, tile:tile + 1], scale=mblk[:, p, 0, tile:tile + 1])\
                       .then_inc(s["exp_done"], 1)
                    if split and st % 2 == 0 and st >= 8:
                        if st == 8:
                            act.wait_ge(ctx_in[p], 8 * b + 32 if isinstance(b, int) else (b - p) * 8 + 32)
                            act.wait_ge(s["proj_done"], 8 * (b + 1))
                        split_ctx(p, (st - 8) // 2)

            with act.Fori(0, NBLK - 3, 2) as b:
                x_block(b, 0)
                x_block(b + 1, 1)
            x_block(NBLK - 2, 0, split=False)
            x_block(NBLK - 1, 1, proj=False, split=False)

            act.wait_ge(s["denb_done"], 1)
            for i in range(2):
                last = act.activation(rden[:, 2 * i:2 * i + 2, :], pS[:, i, :].rearrange("p (g q) -> p g q", g=2), ACT.Copy)
            last.then_inc(s["rden_ready"], 1)

            def split_q(m, p):
                act.wait_ge(min_in[p], 16 * (m // 2 + 1) if isinstance(m, int) else 8 * (m - p) + 16)
                act.activation(mwh[:, q_part], mw_in[:, p, q_part], ACT.Copy, scale=SW).then_inc(s["mq_hi"], 1)

            def split_kv(m, p):
                act.wait_ge(min_in[p], 16 * (m // 2 + 1) if isinstance(m, int) else 8 * (m - p) + 16)
                act.activation(mwh[:, kv_part], mw_in[:, p, kv_part], ACT.Copy, scale=SW).then_inc(s["mkv_hi"], 1)

            transposed(2)
            split_q(0, 0)
            split_kv(0, 0)
            act.wait_ge(s["lat_mm"], 1)
            for t in range(TT):
                act.activation(work[:, 0, 0:QLR], pS[:, 2 + t, 0:QLR], ACT.Square, accum_out=ssq[:, t:t + 1]).then_inc(s["ach"], 1)
                act.wait_ge(s["ach"], 2 * t + 1)
                act.activation(work[:, 0, 0:KVLR], pO[:, 0, KVLR * t:KVLR * t + KVLR], ACT.Square,
                               accum_out=ssq[:, TT + t:TT + t + 1]).then_inc(s["ach"], 1)
                act.wait_ge(s["ach"], 2 * t + 2)
            act.nop().then_inc(s["ssq_ready"], 1)

            def mla_exps(m):
                act.wait_ge(s["negmax"], m + 1)
                for j in range(2):
                    for t, (lo, hi) in enumerate(((0, 128), (128, 384))):
                        last = act.activation(pm[:, j, lo:hi], pO[:, j, lo:hi], ACT.Exp, bias=nm[:, t, j:j + 1],
                                              scale=MLA_SCALE, accum_out=sm[:, t, j:j + 1])
                last.then_inc(s["exps_done"], 1)

            def mla_pair(m, p, proj=True, ahead=True):
                mla_exps(m)
                if proj:
                    split_kv(m + 1, 1 - p)
                    mla_evac_q(m + 1, 1 - p)
                act.wait_ge(mout_in[p], 16 * (m // 2 + 1) if isinstance(m, int) else 8 * (m - p) + 16)
                act.activation(woh[:, p], mw_out[:, p], ACT.Copy, scale=SW).then_inc(s["wo_hi"], 1)
                act.wait_ge(s["pt_done"], m + 1)
                act.activation(pt, pO[:, :, 0:384], ACT.Copy).then_inc(s["pt_ready"], 1)
                if ahead:
                    split_q(m + 2, p)
                act.wait_ge(s["o_done"], m + 1)
                for j in range(2):
                    act.activation(ah[:, j], pO[:, j, 0:T], ACT.Copy, scale=SH).then_inc(s["a_hi"], 1)
                if proj:
                    mla_evac_kv(m + 1, 1 - p)

            def mla_evac_q(m, p):
                act.wait_ge(s["mproj_done"], 4 * m + 1)
                act.activation(qn[:, p], pS[:, 0, :].rearrange("p (j t) -> p j t", j=2), ACT.Copy,
                               scale=1.0 / (SA * SW)).then_inc(s["qkv_ready"], 1)

            def mla_evac_kv(m, p):
                act.wait_ge(s["mproj_done"], 4 * m + 3)
                act.activation(kn[:, p], pS[:, 2, :].rearrange("p (j t) -> p j t", j=2), ACT.Copy,
                               scale=1.0 / (SA * SW)).then_inc(s["qkv_ready"], 1)
                act.wait_ge(s["mproj_done"], 4 * m + 4)
                act.activation(vv[:, p], pS[:, 3, :].rearrange("p (j t) -> p j t", j=2), ACT.Copy,
                               scale=1.0 / (SA * SW)).then_inc(s["qkv_ready"], 1)

            for c in range(QC + 1):
                act.wait_ge(s["lat_ready"], c + 1)
                act.activation(lath[:, c], lat[:, c], ACT.Copy, scale=SA).then_inc(s["lat_hi"], 1)
            mla_evac_q(0, 0)
            act.wait_ge(s["mproj_done"], 2)
            split_q(1, 1)
            mla_evac_kv(0, 0)
            def split_unit(n, slot):
                act.activation(uwh[:, slot], uw32[:, slot], ACT.Copy, scale=SW).then_inc(s["unit_hi"], 1)

            with act.Fori(0, PAIRS - 3, 2) as m:
                mla_pair(m, 0)
                mla_pair(m + 1, 1)
            act.wait_ge(unit_in[0], 16)
            split_unit(0, 0)
            mla_pair(PAIRS - 2, 0, ahead=False)
            act.wait_ge(unit_in[1], 16)
            split_unit(1, 1)
            mla_pair(PAIRS - 1, 1, proj=False, ahead=False)
            act.wait_ge(unit_in[2], 16)
            split_unit(2, 2)

            def hidden(n, bank, buf):
                act.wait_ge(s["gu_done"], n + 1)
                act.activation(sg[:, buf], pS[:, bank, 0:T], ACT.Silu, scale=1.0 / (SA * SW)).then_inc(s["silu_ready"], 1)

            transposed(3)
            act.wait_ge(s["xT_ready"], 3)
            for c in range(HC):
                last = act.activation(xh[:, c], xT[:, c, :], ACT.Copy, scale=SA)
            last.then_inc(s["xh_ready"], 1)
            act.wait_ge(s["ntop_ready"], 1)
            for t in range(TT):
                last = act.activation(ex[:, t], lm[:, t], ACT.Exp, bias=ntop[:, t:t + 1])
            last.then_inc(s["ex_ready"], 1)
            hidden(0, 0, 0)

            def moe_units(it, last_turn=False):
                for u in range(UNROLL):
                    n = UNROLL * it + u
                    if not (last_turn and u + 1 >= UNROLL):
                        hidden(n + 1, (u + 1) % 3, (u + 1) % 2)
                    if not (last_turn and u + AHEAD >= UNROLL):
                        slot = (u + AHEAD) % RING
                        act.wait_ge(unit_in[slot], 16 * (UNROLL // RING * it + (u + AHEAD) // RING + 1))
                        act.wait_ge(s["down_done"], n + 1)
                        split_unit(n + AHEAD, slot)

            with act.Fori(0, UNITS // UNROLL - 1) as it:
                moe_units(it)
            moe_units(UNITS // UNROLL - 1, last_turn=True)

        @block.vector
        def _(dve):
            chain = [0]

            def link(ins):
                chain[0] += 1
                ins.then_inc(s["dch"], 1)
                dve.wait_ge(s["dch"], chain[0])

            def norm_stats(src, k, eps):
                for t in range(TT):
                    link(dve.bn_stats(bn[:, t, :], src[:, t, :]))
                    link(dve.bn_aggr(mv[:, t, :], bn[:, t, :]))
                dve.tensor_scalar(var[:, :], mv[:, :, 1], eps, None, ALU.add).then_inc(s["var_ready"], 1)
                dve.wait_ge(s["rstd_ready"], k)

            def norm(src, dst, k, eps=1e-5):
                norm_stats(src, k, eps)
                for t in range(TT):
                    last = dve.tensor_scalar(dst[:, t, :], src[:, t, :], mv[:, t, 0:1], rstd[:, t:t + 1],
                                             ALU.subtract, ALU.mult)
                return last

            dve.wait_ge(s["x_in"], 16)
            norm(x_sb, xn, 1).then_inc(s["xn_ready"], 1)
            def split_ctx(b, p, c):
                dve.wait_ge(s["ctx_hi"], 4 * b + c + 1)
                dve.scalar_tensor_tensor(clo[:, p, c], cbuf[:, p, c], SA, chi[:, p, c],
                                         ALU.mult, ALU.subtract).then_inc(s["ctx_lo"], 1)

            dve.wait_ge(s["wk_hi"], 1)
            dve.scalar_tensor_tensor(wk16[:, 1], wk32, SW, wk16[:, 0], ALU.mult, ALU.subtract).then_inc(s["wk_lo"], 1)
            dve.wait_ge(s["small_in"], 16 * 6)
            link(dve.tensor_scalar(xb[:, 0:2, :], xb[:, 0:2, :], SA, None, ALU.mult))
            mview = mask_i[:, :].rearrange("p (b t) -> p b t", t=CT)
            dve.tensor_scalar(mtab[:, :, 0, :], mview, 0.5, X_SCALE / (SA * SA), ALU.is_gt, ALU.mult)
            link(dve.tensor_scalar(mtab[:, :, 1, :], mview, 0.5, None, ALU.is_gt))
            link(dve.tensor_scalar(mtab[:, :, 1, :], mtab[:, :, 1, :], 1.0, 50.0, ALU.subtract, ALU.mult))
            link(dve.tensor_scalar(rs[:, :], rs[:, :], 0.0, 0.3, ALU.max, ALU.min))
            dve.nop().then_inc(s["prep_ready"], 1)
            for c in range(HC):
                split_ctx(0, 0, c)
            dve.wait_ge(s["q_f"], 1)
            for g in range(HC):
                dve.tensor_copy(qh[:, g], q_f32(probs, g)).then_inc(s["q_hi"], 1)
            for g in range(HC):
                dve.wait_ge(s["q_hi"], g + 1)
                last = dve.tensor_tensor(ql[:, g], q_f32(probs, g), qh[:, g], ALU.subtract)
            last.then_inc(s["q_lo"], 1)
            dve.wait_ge(s["wk_hi"], 2)
            dve.scalar_tensor_tensor(wv16[:, 1], wv32, SW, wv16[:, 0], ALU.mult, ALU.subtract).then_inc(s["wk_lo"], 1)

            def split_k(b, n, first=False):
                if n == 0 and not first:
                    dve.wait_ge(s["k_stacked"], 16 * STACK_DMAS * b)
                dve.wait_ge(s["proj_evac"], 8 * b + n + 1)
                dve.tensor_copy(kh[:, n], kf[:, n % 2]).then_inc(s["k_hi"], 1)
                dve.wait_ge(s["k_hi"], 4 * b + n + 1)
                dve.tensor_tensor(kl[:, n], kf[:, n % 2], kh[:, n], ALU.subtract).then_inc(s["k_lo"], 1)

            for n in range(HC):
                split_k(0, n, first=True)
            for c in range(HC):
                split_ctx(1, 1, c)
            dve.wait_ge(s["row_in"], 48)
            dve.tensor_scalar(bo_b[:, :], bo_b[:, :], rs[:, 0:1], None, ALU.mult)
            for t in range(TT):
                last = dve.tensor_tensor(x_sb[:, t, :], x_sb[:, t, :], bet_b[:, :], ALU.add)
            link(last)

            LO, HI = float(np.exp(np.float32(-50.0))), float(np.exp(np.float32(50.0)))

            def x_block(b, p, proj=True, split=True):
                for st in range(STEPS):
                    if proj and st % 2 and st // 2 < HC:
                        split_k(b + 1, st // 2)
                    dve.wait_ge(s["exp_done"], STEPS * b + st + 1)
                    g, tile = st // CT, st % CT
                    dve.tensor_scalar(probs[:, tile], probs[:, tile], LO, HI, ALU.max, ALU.min)\
                       .then_inc(s["clip_done"], 1)
                    if tile:
                        dve.wait_ge(s["clip_done"], STEPS * b + st + 1)
                        if tile == 1:
                            dve.wait_ge(s["dsum_done"], HC * b + g + 1)
                        else:
                            dve.wait_ge(s["sum_done"], 12 * b + 3 * g + tile - 1)
                        dve.tensor_tensor(psum4, probs[:, 0] if tile == 1 else psum4, probs[:, tile], ALU.add)\
                           .then_inc(s["sum_done"], 1)
                    if split and st % 2 == 0 and st >= 8:
                        if st == 8:
                            dve.wait_ge(s["proj_done"], 8 * (b + 1))
                        split_ctx(b + 2, p, (st - 8) // 2)

            with dve.Fori(0, NBLK - 3, 2) as b:
                x_block(b, 0)
                x_block(b + 1, 1)
            x_block(NBLK - 2, 0, split=False)
            x_block(NBLK - 1, 1, proj=False, split=False)

            dve.wait_ge(s["x_acc_done"], 1)
            link(dve.tensor_scalar(den, pD[:, 0:T], 1e-30, None, ALU.max))
            dve.reciprocal(den, den).then_inc(s["den_ready"], 1)
            dve.wait_ge(s["rden_ready"], 1)
            for i in range(2):
                last = dve.tensor_tensor(ctxn[:, 2 * i:2 * i + 2, :], pO[:, i, :].rearrange("p (g q) -> p g q", g=2),
                                         rden[:, 2 * i:2 * i + 2, :], ALU.mult)
            link(last)
            for g in range(HC):
                last = dve.tensor_scalar(ctxn[:, g], ctxn[:, g], xb[:, 2, g:g + 1], None, ALU.add)
            last.then_inc(s["ctxn_ready"], 1)
            for t in range(TT):
                dve.wait_ge(s["delta_done"], t + 1)
                link(dve.scalar_tensor_tensor(work[:, t, :], pS[:, 2 + t, :], rs[:, 0:1], bo_b[:, :], ALU.mult, ALU.add))
            norm_stats(work, 2, 1e-5)
            for t in range(TT):
                link(dve.scalar_tensor_tensor(work[:, t, :], work[:, t, :], mv[:, t, 0:1], gam_b[:, :],
                                              ALU.subtract, ALU.mult))
                link(dve.scalar_tensor_tensor(x1_sb[:, t, :], work[:, t, :], rstd[:, t:t + 1], x_sb[:, t, :],
                                              ALU.mult, ALU.add))

            def split_q(m, p):
                dve.wait_ge(s["mq_hi"], m + 1)
                dve.scalar_tensor_tensor(mwl[:, q_part], mw_in[:, p, q_part], SW, mwh[:, q_part], ALU.mult, ALU.subtract)\
                   .then_inc(s["mq_lo"], 1)

            def split_kv(m, p):
                dve.wait_ge(s["mkv_hi"], m + 1)
                dve.scalar_tensor_tensor(mwl[:, kv_part], mw_in[:, p, kv_part], SW, mwh[:, kv_part], ALU.mult, ALU.subtract)\
                   .then_inc(s["mkv_lo"], 1)

            norm(x1_sb, xn, 3).then_inc(s["xn_ready"], 1)
            split_q(0, 0)
            split_kv(0, 0)
            dve.wait_ge(s["zc_ready"], 1)
            link(dve.tensor_copy(o2n_f, o2n_r[:, :]))
            link(dve.tensor_scalar(keep, o2n_f, -1.0, None, ALU.not_equal))
            link(dve.tensor_scalar(nkeep, keep, 1.0, -NEG, ALU.subtract, ALU.mult))
            link(dve.tensor_copy(o2n_cf, o2n_c[:, :]))
            link(dve.tensor_copy(iota_f, iota_i[:, :]))
            link(dve.tensor_scalar(emap, iota_f, o2n_cf, None, ALU.is_equal))
            dve.wait_ge(s["ssq_ready"], 1)
            link(dve.tensor_scalar(ssq[:, 0:TT], ssq[:, 0:TT], 1.0 / QLR, 1e-6, ALU.mult, ALU.add))
            dve.tensor_scalar(ssq[:, TT:2 * TT], ssq[:, TT:2 * TT], 1.0 / KVLR, 1e-6, ALU.mult, ALU.add)\
               .then_inc(s["lvar_ready"], 1)
            dve.wait_ge(s["lrstd_ready"], 1)
            for t in range(TT):
                dve.tensor_scalar(cqn[:, t], pS[:, 2 + t, 0:QLR], lrs[:, t:t + 1], None, ALU.mult)
                last = dve.tensor_scalar(kvn[:, t], pO[:, 0, KVLR * t:KVLR * t + KVLR], lrs[:, TT + t:TT + t + 1], None, ALU.mult)
            last.then_inc(s["latn_ready"], 1)
            dve.wait_ge(s["rope_in"], 32)
            link(dve.tensor_tensor(rp1, pO[:, 1, 0:T], cosT[:, :], ALU.mult))
            link(dve.tensor_tensor(rp2, pO[:, 1, T:2 * T], sinT[:, :], ALU.mult))
            link(dve.tensor_tensor(kpe, rp1, rp2, ALU.add))
            dve.nop().then_inc(s["kpe_ready"], 1)
            dve.wait_ge(s["lat_tr"], 1)
            for c in range(QC + 1):
                dve.tensor_scalar(lat[:, c], pS[:, c // 2, 256 * (c % 2):256 * (c % 2) + 256], lnw[:, c:c + 1], None, ALU.mult)\
                   .then_inc(s["lat_ready"], 1)
            for c in range(QC + 1):
                dve.wait_ge(s["lat_hi"], c + 1)
                dve.scalar_tensor_tensor(latl[:, c], lat[:, c], SA, lath[:, c], ALU.mult, ALU.subtract).then_inc(s["lat_lo"], 1)

            def rope_q(m, p):
                dve.wait_ge(s["mproj_done"], 4 * m + 2)
                dve.scalar_tensor_tensor(rp1, pS[:, 1, 0:T], 1.0 / (SA * SW), cosT[:, :], ALU.mult, ALU.mult).then_inc(s["rope_step"], 1)
                dve.scalar_tensor_tensor(rp2, pS[:, 1, T:2 * T], 1.0 / (SA * SW), sinT[:, :], ALU.mult, ALU.mult).then_inc(s["rope_step"], 1)
                dve.wait_ge(s["rope_step"], 2 * m + 2)
                dve.tensor_tensor(qpe[:, p], rp1, rp2, ALU.add).then_inc(s["rope_ready"], 1)

            diag = pO[:, :, 0:384].rearrange("p j (b k) -> p j b k", k=128)

            def mla_pair(m, p, proj=True, ahead=True):
                dve.wait_ge(s["s_done"], m + 1)
                for j in range(2):
                    last = dve.tensor_tensor(diag[:, j, 0:3:2, :], diag[:, j, 0:3:2, :],
                                             cmask[:, :].unsqueeze(1).broadcast_to([128, 2, 128]), ALU.add)
                last.then_inc(s["masked"], 1)
                dve.wait_ge(s["masked"], m + 1)
                dve.reduce_max(mx[:, 0, :], pO[:, :, 0:128], AX.X)
                dve.reduce_max(mx[:, 1, :], pO[:, :, 128:384], AX.X).then_inc(s["maxed"], 1)
                dve.wait_ge(s["maxed"], m + 1)
                dve.tensor_scalar(nm, mx, -MLA_SCALE, None, ALU.mult).then_inc(s["negmax"], 1)
                dve.wait_ge(s["exps_done"], m + 1)
                dve.reciprocal(rc, sm).then_inc(s["rec_ready"], 1)
                dve.wait_ge(s["rec_ready"], m + 1)
                for j in range(2):
                    for t, (lo, hi) in enumerate(((0, 128), (128, 384))):
                        last = dve.tensor_scalar(pm[:, j, lo:hi], pm[:, j, lo:hi], rc[:, t, j:j + 1], None, ALU.mult)
                last.then_inc(s["p_ready"], 1)
                if proj:
                    rope_q(m + 1, 1 - p)
                    split_kv(m + 1, 1 - p)
                dve.wait_ge(s["wo_hi"], m + 1)
                dve.scalar_tensor_tensor(wol[:, p], mw_out[:, p], SW, woh[:, p], ALU.mult, ALU.subtract)\
                   .then_inc(s["wo_lo"], 1)
                for j in range(2):
                    dve.wait_ge(s["a_hi"], 2 * m + 1 + j)
                    dve.scalar_tensor_tensor(al[:, j], pO[:, j, 0:T], SH, ah[:, j], ALU.mult, ALU.subtract)\
                       .then_inc(s["a_lo"], 1)
                if ahead:
                    split_q(m + 2, p)

            def split_unit(n, slot):
                dve.wait_ge(s["unit_hi"], n + 1)
                dve.scalar_tensor_tensor(uwl[:, slot], uw32[:, slot], SW, uwh[:, slot],
                                         ALU.mult, ALU.subtract).then_inc(s["unit_lo"], 1)

            rope_q(0, 0)
            split_q(1, 1)
            with dve.Fori(0, PAIRS - 3, 2) as m:
                mla_pair(m, 0)
                mla_pair(m + 1, 1)
            split_unit(0, 0)
            mla_pair(PAIRS - 2, 0, ahead=False)
            split_unit(1, 1)
            mla_pair(PAIRS - 1, 1, proj=False, ahead=False)
            split_unit(2, 2)
            dve.wait_ge(s["mla_done"], 1)
            link(dve.scalar_tensor_tensor(x1_sb[:, 0, :], pD[:, :], 1.0 / (SH * SW), x1_sb[:, 0, :], ALU.mult, ALU.add))
            link(dve.scalar_tensor_tensor(x1_sb[:, 1, :], pP[:, :], 1.0 / (SH * SW), x1_sb[:, 1, :], ALU.mult, ALU.add))

            norm(x1_sb, xn, 4).then_inc(s["xn_ready"], 1)
            dve.wait_ge(s["xh_ready"], 1)
            for c in range(HC):
                last = dve.scalar_tensor_tensor(xl[:, c], xT[:, c, :], SA, xh[:, c], ALU.mult, ALU.subtract)
            last.then_inc(s["xl_ready"], 1)
            dve.wait_ge(s["logits_done"], 1)
            for t in range(TT):
                link(dve.tensor_tensor(lm[:, t], pO[:, t, 0:NEXP], keep, ALU.mult))
                link(dve.tensor_tensor(lm[:, t], lm[:, t], nkeep, ALU.add))
                link(dve.max(top[:, t], lm[:, t]))
            dve.tensor_scalar(ntop, top[:, :, 0], -1.0, None, ALU.mult).then_inc(s["ntop_ready"], 1)
            for t in range(TT):
                link(dve.match_replace(rep[:, t], top[:, t], lm[:, t], 3.0 * NEG))
            link(dve.tensor_tensor(sel, rep, lm, ALU.not_equal))
            dve.nop().then_inc(s["sel_ready"], 1)
            dve.wait_ge(s["ex_ready"], 1)
            link(dve.tensor_tensor(ex, ex, sel, ALU.mult))
            link(dve.reduce_sum(zs, ex, AX.X))
            link(dve.reciprocal(zr, zs))
            link(dve.tensor_scalar(zr, zr, SH / (SA * SW), None, ALU.mult))
            dve.wait_ge(s["cnt_done"], 1)
            for t in range(TT):
                link(dve.tensor_scalar(rep[:, t], pO[:, t, 256:256 + NEXP], float(CAP), zr[:, t:t + 1], ALU.is_le, ALU.mult))
                link(dve.tensor_tensor(ex[:, t], ex[:, t], rep[:, t], ALU.mult))
            dve.nop().then_inc(s["w_ready"], 1)
            dve.wait_ge(s["wt_done"], 1)
            dve.tensor_copy(wT, pS[:, 2, 0:T]).then_inc(s["wt_ready"], 1)
            dve.wait_ge(s["wn_done"], 1)
            dve.tensor_copy(wnew[0:KEPT, :], pS[0:KEPT, 3, 0:T]).then_inc(s["wn_ready"], 1)

            def hidden(n, loads, slot, bank, buf):
                dve.wait_ge(s["silu_ready"], n + 1)
                dve.tensor_tensor(m1[:, buf], pS[:, bank, T:2 * T], sg[:, buf], ALU.mult).then_inc(s["m1_ready"], 1)
                dve.wait_ge(wb_in[slot], 32 * loads)
                dve.wait_ge(s["m1_ready"], n + 1)
                dve.tensor_tensor(m2[:, buf], m1[:, buf], wb[:, slot], ALU.mult).then_inc(s["m2_ready"], 1)
                dve.wait_ge(s["m2_ready"], n + 1)
                dve.tensor_copy(hh[:, buf], m2[:, buf]).then_inc(s["h_hi"], 1)
                dve.wait_ge(s["h_hi"], n + 1)
                dve.tensor_tensor(hl[:, buf], m2[:, buf], hh[:, buf], ALU.subtract).then_inc(s["h_lo"], 1)

            hidden(0, 1, 0, 0, 0)

            def moe_units(it, last_turn=False):
                for u in range(UNROLL):
                    n = UNROLL * it + u
                    if not (last_turn and u + 1 >= UNROLL):
                        hidden(n + 1, UNROLL // RING * it + (u + 1) // RING + 1, (u + 1) % RING, (u + 1) % 3, (u + 1) % 2)
                    if not (last_turn and u + AHEAD >= UNROLL):
                        dve.wait_ge(s["down_done"], n + 1)
                        split_unit(n + AHEAD, (u + AHEAD) % RING)

            with dve.Fori(0, UNITS // UNROLL - 1) as it:
                moe_units(it)
            moe_units(UNITS // UNROLL - 1, last_turn=True)
            dve.wait_ge(s["moe_done"], 1)
            dve.scalar_tensor_tensor(work[:, 0, :], pD[:, :], 1.0 / (SH * SW), x1_sb[:, 0, :], ALU.mult, ALU.add)
            dve.scalar_tensor_tensor(work[:, 1, :], pP[:, :], 1.0 / (SH * SW), x1_sb[:, 1, :], ALU.mult, ALU.add)\
               .then_inc(s["out_ready"], 1)

        @block.tensor
        def _(pe):
            def mm(o, lhsT, rhs, start, stop, **kw):
                return pe.matmul(o, lhsT, rhs, start=start, stop=stop, **kw)

            def add_zero(banks, start, stop):
                for o in banks:
                    last = mm(o, zero16[:, 0:128], zero16[:, :], start, stop, skip_group_check=True)
                return last

            def transpose_rows(k):
                pe.wait_ge(s["xn_ready"], k)
                for t in range(TT):
                    for c in range(HC):
                        last = pe.transpose(pS[:, c // 2, 256 * (c % 2) + 128 * t:256 * (c % 2) + 128 * t + 128],
                                            xn[:, t, 128 * c:128 * c + 128], ident[:, :])
                last.then_inc(s["tr_done"], 1)

            pe.wait_ge(s["const_ready"], 1)
            transpose_rows(1)
            pe.wait_ge(s["wq_in"], 16)
            pe.wait_ge(s["xT_ready"], 1)
            for g in range(HC):
                for c in range(HC):
                    last = mm(pS[:, 2 + g // 2, 256 * (g % 2):256 * (g % 2) + 256], wqT[:, c, 128 * g:128 * g + 128],
                              xT[:, c, :], c == 0, c == HC - 1)
            last.then_inc(s["q_mm"], 1)

            def project(b, p, n, first=False):
                if n == 0:
                    pe.wait_ge(s["ctx_lo"], 4 * (b + 1))
                if first and n in (0, HC):
                    pe.wait_ge(s["wk_lo"], 1 + n // HC)
                if not (first and n == 0):
                    pe.wait_ge(s["proj_evac"], 8 * b + n)
                k = 0
                for c in range(HC):
                    for wi, ci in ((0, chi), (1, chi), (0, clo)):
                        if n < HC:
                            last = mm(pP[:, :], wk16[:, wi, c, 128 * n:128 * n + 128], ci[:, p, c, :], k == 0, k == 11)
                        else:
                            r = n - HC
                            last = mm(pP[:, :], ci[:, p, c, 128 * r:128 * r + 128], wv16[:, wi, c, :], k == 0, k == 11)
                        k += 1
                last.then_inc(s["proj_done"], 1)

            for n in range(8):
                project(0, 0, n, first=True)
            add_zero((pO[:, 0, :], pO[:, 1, :], pD[:, :]), True, False).then_inc(s["dsum_done"], 1)

            def scores(b, p, st):
                g, tile = st // CT, st % CT
                if st >= 2:
                    pe.wait_ge(s["exp_done"], STEPS * b + st - 1)
                for j in range(4):
                    last = mm(step_scores(st)[:, j, :], k_st[:, p, j, g, 128 * tile:128 * tile + 128],
                              q_st[:, j, g, :], True, True)
                last.then_inc(s["scores_done"], 1)

            def weigh(b, p, st):
                g, tile = st // CT, st % CT
                if g == 0:
                    pe.wait_ge(s["proj_evac"], 8 * b + HC + tile + 1)
                pe.wait_ge(s["clip_done"], STEPS * b + st + 1)
                for j in range(4):
                    last = mm(pO[32 * j:32 * j + 32, g // 2, 256 * (g % 2):256 * (g % 2) + 256],
                              v_sb[:, p, tile, 128 * g + 32 * j:128 * g + 32 * j + 32], probs[:, tile, j, :], False, False,
                              skip_group_check=True)

            def add_sums(b, g):
                pe.wait_ge(s["sum_done"], 12 * b + 3 * g + 3)
                for j in range(4):
                    last = mm(pD[32 * j:32 * j + 32, 0:T], onecol[:, g, :], psum4[:, j, :], False, False,
                              skip_group_check=True)
                last.then_inc(s["dsum_done"], 1)

            def x_block(b, p, proj=True):
                pe.wait_ge(s["k_stacked"], 16 * STACK_DMAS * (b + 1))
                for st in range(STEPS):
                    scores(b, p, st)
                    if proj and st % 2 == 0:
                        project(b + 1, 1 - p, st // 2)
                    if st:
                        weigh(b, p, st - 1)
                    if st and st % CT == 1 and st > CT:
                        add_sums(b, st // CT - 1)
                weigh(b, p, STEPS - 1)
                add_sums(b, HC - 1)

            pe.wait_ge(s["q_stacked"], 16 * 16)
            with pe.Fori(0, NBLK - 3, 2) as b:
                x_block(b, 0)
                x_block(b + 1, 1)
            x_block(NBLK - 2, 0)
            x_block(NBLK - 1, 1, proj=False)
            add_zero((pO[:, 0, :], pO[:, 1, :], pD[:, :]), False, True).then_inc(s["x_acc_done"], 1)

            pe.wait_ge(s["zc_ready"], 1)
            pe.wait_ge(s["den_ready"], 1)
            for g in range(HC):
                last = mm(pS[:, g // 2, 256 * (g % 2):256 * (g % 2) + 256], selrow[:, g, :], den, True, True)
            last.then_inc(s["denb_done"], 1)
            pe.wait_ge(s["ctxn_ready"], 1)
            pe.wait_ge(s["wo_in"], 16)
            for t in range(TT):
                for g in range(HC):
                    last = mm(pS[:, 2 + t, :], ctxn[:, g, 128 * t:128 * t + 128], woT[:, g, :], g == 0, g == HC - 1)
                last.then_inc(s["delta_done"], 1)

            transpose_rows(2)
            pe.wait_ge(s["xT_ready"], 2)
            pe.wait_ge(s["qa_in"], 16)
            pe.wait_ge(s["kva_in"], 16)
            for t in range(TT):
                for c in range(HC):
                    mm(pS[:, 2 + t, 0:QLR], xT[:, c, 128 * t:128 * t + 128], wqaT[:, c, :], c == 0, c == HC - 1)
                for c in range(HC):
                    mm(pO[:, 0, KVLR * t:KVLR * t + KVLR], xT[:, c, 128 * t:128 * t + 128], wkvaT[:, c, 0:KVLR],
                       c == 0, c == HC - 1)
            for r in range(2):
                for c in range(HC):
                    last = mm(pO[:, 1, T * r:T * r + T], wkvaT[:, c, KVLR + 128 * r:KVLR + 128 * r + 128], xT[:, c, :],
                              c == 0, c == HC - 1)
            last.then_inc(s["lat_mm"], 1)
            pe.wait_ge(s["latn_ready"], 1)
            for t in range(TT):
                for c in range(QC + 1):
                    src = cqn[:, t, 128 * c:128 * c + 128] if c < QC else kvn[:, t, :]
                    last = pe.transpose(pS[:, c // 2, 256 * (c % 2) + 128 * t:256 * (c % 2) + 128 * t + 128], src, ident[:, :])
            last.then_inc(s["lat_tr"], 1)
            pe.wait_ge(s["kpe_ready"], 1)
            add_zero((pD[:, :], pP[:, :]), True, False)

            PARTS = ((mwh, lath), (mwl, lath), (mwh, latl))

            def proj_q(m, first=False):
                if not first:
                    pe.wait_ge(s["qkv_ready"], 3 * m)
                    pe.wait_ge(s["rope_ready"], m)
                pe.wait_ge(s["mq_lo"], m + 1)
                for r in range(2):
                    for j in range(2):
                        for c in range(QC):
                            if first and r == 0 and j == 0:
                                pe.wait_ge(s["lat_lo"], c + 1)
                            at = 512 * c + 256 * r + 128 * j
                            for k, (w, x) in enumerate(PARTS):
                                last = mm(pS[:, r, T * j:T * j + T], w[:, at:at + 128], x[:, c, :],
                                          c == 0 and k == 0, c == QC - 1 and k == 2)
                    last.then_inc(s["mproj_done"], 1)

            def proj_k(m):
                pe.wait_ge(s["mkv_lo"], m + 1)
                for j in range(2):
                    at = QC * 512 + 128 * j
                    for k, (w, x) in enumerate(PARTS):
                        last = mm(pS[:, 2, T * j:T * j + T], w[:, at:at + 128], x[:, QC, :], k == 0, k == 2)
                last.then_inc(s["mproj_done"], 1)

            def proj_v():
                for t in range(TT):
                    for k, (w, x) in enumerate(PARTS):
                        last = mm(pS[:, 3, T * t:T * t + T], x[:, QC, 128 * t:128 * t + 128],
                                  w[:, QC * 512 + 256:QC * 512 + 512], k == 0, k == 2)
                last.then_inc(s["mproj_done"], 1)

            def out_product(m, p, t):
                if t == 0:
                    pe.wait_ge(s["wo_lo"], m + 1)
                for j in range(2):
                    for x, w in ((ah, woh), (ah, wol), (al, woh)):
                        mm((pD, pP)[t][:, :], x[:, j, 128 * t:128 * t + 128], w[:, p, HID * j:HID * j + HID],
                           False, False, skip_group_check=True)

            def mla_scores(m, p):
                pe.wait_ge(s["qkv_ready"], 3 * m + 2)
                pe.wait_ge(s["rope_ready"], m + 1)
                for j in range(2):
                    for t, (lo, hi) in enumerate(((0, 128), (128, 384))):
                        mm(pO[:, j, lo:hi], qn[:, p, j, 128 * t:128 * t + 128], kn[:, p, j, 0:hi - lo], True, False)
                        last = mm(pO[:, j, lo:hi], qpe[64 * j:64 * j + 64, p, 128 * t:128 * t + 128],
                                  kpe[64 * j:64 * j + 64, 0:hi - lo], False, True)
                last.then_inc(s["s_done"], 1)

            def mla_pair(m, p, proj=True, before=True):
                mla_scores(m, p)
                if proj:
                    proj_q(m + 1)
                if before:
                    out_product(m - 1, 1 - p, 0)
                pe.wait_ge(s["p_ready"], m + 1)
                for j in range(2):
                    for i in range(3):
                        last = pe.transpose(pO[:, j, 128 * i:128 * i + 128], pm[:, j, 128 * i:128 * i + 128], ident[:, :])
                last.then_inc(s["pt_done"], 1)
                if before:
                    out_product(m - 1, 1 - p, 1)
                pe.wait_ge(s["pt_ready"], m + 1)
                pe.wait_ge(s["qkv_ready"], 3 * m + 3)
                for j in range(2):
                    mm(pO[:, j, 0:T], vv[:, p, 0, 128 * j:128 * j + 128], pt[:, j, 0:T], True, False)
                    last = mm(pO[:, j, 128:T], vv[:, p, 1, 128 * j:128 * j + 128], pt[:, j, T:384], False, True)
                last.then_inc(s["o_done"], 1)
                if proj:
                    proj_k(m + 1)
                    proj_v()
                pe.wait_ge(s["a_lo"], 2 * m + 2)

            proj_q(0, first=True)
            pe.wait_ge(s["lat_lo"], QC + 1)
            proj_k(0)
            proj_v()
            mla_pair(0, 0, before=False)
            with pe.Fori(1, PAIRS - 2, 2) as m:
                mla_pair(m, 1)
                mla_pair(m + 1, 0)
            mla_pair(PAIRS - 1, 1, proj=False)
            for t in range(TT):
                out_product(PAIRS - 1, 1, t)
            add_zero((pD[:, :], pP[:, :]), False, True).then_inc(s["mla_done"], 1)

            transpose_rows(3)
            pe.wait_ge(s["xT_ready"], 3)
            pe.wait_ge(s["gate_in"], 16)
            for t in range(TT):
                for c in range(HC):
                    last = mm(pO[:, t, 0:NEXP], xT[:, c, 128 * t:128 * t + 128], gateT[:, c, :], c == 0, c == HC - 1)
            last.then_inc(s["logits_done"], 1)
            add_zero((pD[:, :], pP[:, :]), True, False).then_inc(s["down_done"], 1)

            def gate_up(n, bank, ring):
                pe.wait_ge(s["unit_lo"], n + 1)
                for half in range(2):
                    k = 0
                    for c in range(HC):
                        for w, x in ((uwh, xh), (uwl, xh), (uwh, xl)):
                            last = mm(pS[:, bank, T * half:T * half + T],
                                      w[:, ring, 256 * c + 128 * half:256 * c + 128 * half + 128], x[:, c, :], k == 0, k == 11)
                            k += 1
                last.then_inc(s["gu_done"], 1)

            def down(n, ring, buf):
                pe.wait_ge(s["h_lo"], n + 1)
                for t, o in enumerate((pD, pP)):
                    for h, w in ((hh, uwh), (hh, uwl), (hl, uwh)):
                        last = mm(o[:, :], h[:, buf, 128 * t:128 * t + 128], w[:, ring, HC * 256:UW], False, False,
                                  skip_group_check=True)
                last.then_inc(s["down_done"], 1)

            pe.wait_ge(s["xl_ready"], 1)
            gate_up(0, 0, 0)
            pe.wait_ge(s["sel_ready"], 1)
            mm(pO[:, 0, 256:256 + NEXP], tri[:, :], sel[:, 0], True, True)
            mm(pO[:, 1, 256:256 + NEXP], ones[:, :], sel[:, 0], True, False)
            mm(pO[:, 1, 256:256 + NEXP], tri[:, :], sel[:, 1], False, True).then_inc(s["cnt_done"], 1)
            pe.wait_ge(s["w_ready"], 1)
            for t in range(TT):
                last = pe.transpose(pS[:, 2, 128 * t:128 * t + 128], ex[:, t], ident[:, :])
            last.then_inc(s["wt_done"], 1)
            pe.wait_ge(s["wt_ready"], 1)
            mm(pS[0:KEPT, 3, 0:T], emap, wT, True, True).then_inc(s["wn_done"], 1)

            def moe_units(it, last_turn=False):
                for u in range(UNROLL):
                    n = UNROLL * it + u
                    if not (last_turn and u + 1 >= UNROLL):
                        gate_up(n + 1, (u + 1) % 3, (u + 1) % RING)
                    down(n, u % RING, u % 2)

            with pe.Fori(0, UNITS // UNROLL - 1) as it:
                moe_units(it)
            moe_units(UNITS // UNROLL - 1, last_turn=True)
            add_zero((pD[:, :], pP[:, :]), False, True).then_inc(s["moe_done"], 1)


def q_f32(probs, g):
    return probs[:, g // 2, 2 * (g % 2), :]


def kernel(**inputs):
    import numpy as _np
    import concourse.bacc as _bacc
    from concourse import mybir as _mybir
    from concourse.bass_utils import run_bass_kernel_spmd as _run

    v = {k: _np.asarray(t) for k, t in inputs.items()}

    def chunked(wT):
        return wT.reshape(-1, 128, wT.shape[1]).transpose(1, 0, 2)

    def by_channel(vec):
        return vec.reshape(-1, 128).T

    P = "L0_xattn_"
    A = "L0_attn_"
    F = "L0_ffn_"
    arrays = {
        "x": v["x"][0].reshape(TT, 128, HID).transpose(1, 0, 2),
        "ctxT": v["ctx_2048"][0].reshape(NBLK, CB, HC, 128).transpose(0, 3, 2, 1),
        "mask": v["mask_BxS2_ik0"][0].reshape(S2 // 128, 128).T,
        "wqT": chunked(v[P + "Wq"].T), "wkT": chunked(v[P + "Wk"].T), "wvT": chunked(v[P + "Wv"].T),
        "woT": chunked(v[P + "Wo"].T),
        "xb": _np.stack([by_channel(v[P + b]) for b in ("bq", "bk", "bv")], axis=1),
        "bo": v[P + "bo"][None], "gamma": v[P + "ln_gamma"][None], "beta": v[P + "ln_beta"][None],
        "rs": v[P + "residual_scale"].reshape(1, 1),
        "wqaT": chunked(v[A + "w_qa"].T),
        "lnw": _np.concatenate([by_channel(v[A + "q_a_ln_w"]), by_channel(v[A + "kv_a_ln_w"])], axis=1),
        "gateT": chunked(v[F + "gate_weight"].T),
        "o2n_c": v[F + "old_to_new"].reshape(NEXP, 1), "o2n_r": v[F + "old_to_new"].reshape(1, NEXP),
    }
    half = DR // 2
    swap = _np.r_[half:DR, 0:half]
    pe_rows = v[A + "w_kva"][KVLR:]
    arrays["wkvaT"] = chunked(_np.concatenate(
        [v[A + "w_kva"][:KVLR], pe_rows, pe_rows, pe_rows[swap], pe_rows[swap]]).T)
    wqb = v[A + "w_qb"].reshape(PAIRS, 2, DN + DR, QLR)
    wkvb = v[A + "w_kvb"].reshape(PAIRS, 2, DN + DV, KVLR)
    qrows = _np.concatenate([wqb[:, 0, :DN], wqb[:, 1, :DN], wqb[:, 0, DN:], wqb[:, 1, DN:],
                             wqb[:, 0, DN:][:, swap], wqb[:, 1, DN:][:, swap]], axis=1)
    kvrows = _np.concatenate([wkvb[:, 0, :DN], wkvb[:, 1, :DN], wkvb[:, 0, DN:], wkvb[:, 1, DN:]], axis=1)
    arrays["mla_in"] = _np.concatenate(
        [qrows.transpose(0, 2, 1).reshape(PAIRS, QC, 128, 512).transpose(0, 2, 1, 3).reshape(PAIRS, 128, QC * 512),
         kvrows.transpose(0, 2, 1)], axis=2)
    arrays["mla_out"] = v[A + "w_o"].T.reshape(PAIRS, 2, 128, HID).transpose(0, 2, 1, 3).reshape(PAIRS, 128, 2 * HID)
    inv = (1.0 / _np.float32(10000.0) ** (_np.arange(0, DR, 2, dtype=_np.float32) / _np.float32(DR))).astype(_np.float32)
    angle = _np.outer(_np.arange(T, dtype=_np.float32), inv).astype(_np.float32).T
    cos, sin = _np.cos(angle), _np.sin(angle)
    arrays["cosT"] = _np.concatenate([cos] * 4)
    arrays["sinT"] = _np.concatenate([-sin, sin] * 2)
    gu = v[F + "gate_up_proj"].reshape(KEPT // 2, 2, 2, INTER, HID)
    dn = v[F + "down_proj"].reshape(KEPT // 2, 2, HID, INTER)
    rows = [gu[:, 0, :, :128], gu[:, 1, :, :128], _np.concatenate([gu[:, 0, :, 128:], gu[:, 1, :, 128:]], axis=2)]
    cols = [dn[:, 0, :, :128], dn[:, 1, :, :128], _np.concatenate([dn[:, 0, :, 128:], dn[:, 1, :, 128:]], axis=2)]
    gu_u = _np.stack(rows, axis=1).reshape(UNITS, 256, HC, 128).transpose(0, 3, 2, 1).reshape(UNITS, 128, HC * 256)
    dn_u = _np.stack(cols, axis=1).reshape(UNITS, HID, 128).transpose(0, 2, 1)
    arrays["units"] = _np.concatenate([gu_u, dn_u], axis=2)

    nc = _bacc.Bacc("TRN2", target_bir_lowering=False, num_devices=1)
    arrays = {k: _np.ascontiguousarray(t) for k, t in arrays.items()}
    aps = {k: nc.dram_tensor("in_" + k, t.shape, _mybir.dt.from_np(t.dtype), kind="ExternalInput").ap()
           for k, t in arrays.items()}
    out = nc.dram_tensor("out_0", (128, TT, HID), _mybir.dt.float32, kind="ExternalOutput").ap()
    build(nc, aps, out)
    r = _run(nc, [{"in_" + k: t for k, t in arrays.items()}], core_ids=[0])
    return r.results[0]["out_0"].transpose(1, 0, 2).reshape(1, T, HID)
```
